# Optimizing a Trainium2 kernel written in Bass

```python
import numpy as np
import jax
import jax.numpy as jnp

def _softmax(x, axis=-1):
    return jax.nn.softmax(x, axis=axis)

def _gelu(x):
    return jax.nn.gelu(x, approximate=True)

def _silu(x):
    return jax.nn.silu(x)

def _sigmoid(x):
    return jax.nn.sigmoid(x)

def _layernorm(x, axis=-1, eps=1e-05):
    m = jnp.mean(x, axis=axis, keepdims=True)
    v = jnp.var(x, axis=axis, keepdims=True)
    return (x - m) / jnp.sqrt(v + eps)

def _scatter_add(tgt, idx, src, axis=0):
    return tgt.at[idx].add(src)

def _segment_sum(src, seg, n):
    return jax.ops.segment_sum(src, seg, n)
kernel_name = 'mk_adj_resnorm_d1_adj_r2_b85545'

def setup_inputs(seed: int=0):
    np.random.seed(seed)
    _w = jnp.asarray

    def _rec_inputs():
        import jax
        import jax.numpy as jnp
        _gk = jax.random.key(seed)
        x = -0.0001538 + 1 * jax.random.normal(jax.random.fold_in(_gk, 1), (64, 128, 384), jnp.float32)
        _w = (1.0 + jnp.arange(128, dtype=jnp.float32)) ** (-0.5)
        _w = _w / _w.mean()
        _pij = jnp.clip(0.015625 * _w[:, None] * _w[None, :], 0.0, 1.0)
        _a = jax.random.uniform(jax.random.fold_in(_gk, 2), (64, 128, 128)) < _pij
        _a = jnp.logical_or(_a, jnp.swapaxes(_a, -1, -2))
        _a = jnp.logical_or(_a, jnp.eye(128, dtype=bool))
        _af = _a.astype(jnp.float32)
        _af = _af * jax.random.uniform(jax.random.fold_in(_gk, 3), (64, 128, 128), jnp.float32, 0.05, 4.42607)
        adj = _af
        return (x, adj)
    x, adj = _rec_inputs()

    def _L0_gnn_setup():
        import jax, jax.numpy as jnp
        import numpy as np
        NUM_HEADS = 12
        HIDDEN = 384
        HEAD = HIDDEN // NUM_HEADS
        SCALE = HIDDEN ** (-0.5)
        key = jax.random.key(seed)
        ks = jax.random.split(key, 8)
        B, N = (16, 256)
        std = HIDDEN ** (-0.5)
        return {'x': jax.random.normal(ks[0], (B, N, HIDDEN), dtype=jnp.float32), 'encoding_bias': jax.random.normal(ks[1], (B, N, N), dtype=jnp.float32), 'Wq': jax.random.normal(ks[2], (HIDDEN, HIDDEN), dtype=jnp.float32) * std, 'Wk': jax.random.normal(ks[3], (HIDDEN, HIDDEN), dtype=jnp.float32) * std, 'Wv': jax.random.normal(ks[4], (HIDDEN, HIDDEN), dtype=jnp.float32) * std, 'bv': jax.random.normal(ks[5], (HIDDEN,), dtype=jnp.float32) * 0.01, 'Wo': jax.random.normal(ks[6], (HIDDEN, HIDDEN), dtype=jnp.float32) * std, 'bo': jax.random.normal(ks[7], (HIDDEN,), dtype=jnp.float32) * 0.01}
    _L0_gnn_all = _L0_gnn_setup()
    _L0_gnn_in = {k: v for k, v in _L0_gnn_all.items() if k in ('Wq', 'Wk', 'Wv', 'bv', 'Wo', 'bo')}
    del _L0_gnn_all
    return {'x': x, 'adj': adj, 'L0_gnn_Wq': _L0_gnn_in['Wq'], 'L0_gnn_Wk': _L0_gnn_in['Wk'], 'L0_gnn_Wv': _L0_gnn_in['Wv'], 'L0_gnn_bv': _L0_gnn_in['bv'], 'L0_gnn_Wo': _L0_gnn_in['Wo'], 'L0_gnn_bo': _L0_gnn_in['bo']}

def reference(x, adj, L0_gnn_Wq, L0_gnn_Wk, L0_gnn_Wv, L0_gnn_bv, L0_gnn_Wo, L0_gnn_bo):
    import jax
    import jax.numpy as jnp

    def _L0_gnn_ref(x, encoding_bias, Wq, Wk, Wv, bv, Wo, bo):
        import jax, jax.numpy as jnp
        import numpy as np
        NUM_HEADS = 12
        HIDDEN = 384
        HEAD = HIDDEN // NUM_HEADS
        SCALE = HIDDEN ** (-0.5)
        B, N, _ = x.shape
        q = (x @ Wq.T).reshape(B, N, NUM_HEADS, HEAD)
        k = (x @ Wk.T).reshape(B, N, NUM_HEADS, HEAD)
        v = (x @ Wv.T + bv).reshape(B, N, NUM_HEADS, HEAD)
        a = jnp.einsum('bnhd,bmhd->bhnm', q, k) * SCALE + encoding_bias[:, None, :, :]
        pad_mask = jnp.all(a == 0, axis=-1)
        a = jnp.where(pad_mask[..., None], -jnp.inf, a)
        a = jax.nn.softmax(a, axis=-1)
        a = jnp.nan_to_num(a)
        o = jnp.einsum('bhnm,bmhd->bnhd', a, v).reshape(B, N, HIDDEN)
        return o @ Wo.T + bo
    x = _layernorm(x + _L0_gnn_ref(x, adj, L0_gnn_Wq, L0_gnn_Wk, L0_gnn_Wv, L0_gnn_bv, L0_gnn_Wo, L0_gnn_bo), axis=-1)
    return x

_drawn_inputs = setup_inputs


def setup_inputs(seed=0):
    import zlib

    import numpy as np

    out = dict(_drawn_inputs(seed))
    spreads = {}
    factors = {'L0_gnn_bv': 5.251, 'L0_gnn_bo': 5.795}
    for name, (base, spread) in spreads.items():
        noise = np.random.default_rng([zlib.crc32(name.encode()), seed]).standard_normal(out[name].shape)
        drawn = base * np.exp(spread * noise) if base else spread * noise
        out[name] = jnp.asarray(drawn.astype(out[name].dtype))
    for name, factor in factors.items():
        out[name] = (out[name] * factor).astype(out[name].dtype)
    return out
```

```python
from contextlib import ExitStack

import concourse.bass as bass
from concourse import mybir

F32 = mybir.dt.float32
F32R = mybir.dt.float32r
ALU = mybir.AluOpType
ACT = mybir.ActivationFunctionType
AX_X = mybir.AxisListType.X

HEADS = 12
EPS = 1e-5
FLOAT_MAX = 3.4028234e38
GB = 4


def graph_attention(nc, x, xT, adj, wqT, wkT, wvT, woT, bv, bo, out):
    GRAPHS, N, HID = x.shape
    P = 128
    HD = HID // HEADS
    HC = P // HD
    NC = HID // P
    GROUPS = GRAPHS // GB
    UNITS = NC * GB
    SCALE = float(HID) ** -0.5
    OUT_BANK = (1, 1, 0, 1)
    A_RING, E_RING, PS_RING = 3, 6, 2
    T_LAG, PV_LAG, O_LAG = 3, 4, 5
    assert N == P and HC * N == 512 and GB * N == 512

    ctx = ExitStack()
    with ctx:
        def sb(name, shape, dt=F32):
            return ctx.enter_context(nc.sbuf_tensor(name, shape, dt))

        def psum(name, shape):
            return ctx.enter_context(nc.psum_tensor(name, shape, F32))

        def sem(name):
            return ctx.enter_context(nc.semaphore(name))

        w_raw = sb("w_raw", [P, 2, NC, HID])
        w_hi = {w: sb(f"w{w}_hi", [P, NC, HID], F32R) for w in "qkvo"}
        w_lo = {w: sb(f"w{w}_lo", [P, NC, HID], F32R) for w in "qkvo"}
        bv_rows = sb("bv_rows", [P, HID])
        bo_rows = sb("bo_rows", [P, HID])
        ident = sb("ident", [P, P])
        zeros = sb("zeros", [P, P])
        neg_half = sb("neg_half", [P, GB])

        xT_raw = sb("xT_raw", [P, NC, GB * N])
        xT_hi = sb("xT_hi", [P, NC, GB * N], F32R)
        xT_lo = sb("xT_lo", [P, NC, GB * N], F32R)
        adj_raw = sb("adj_raw", [P, GB, N])
        neg_adj = sb("neg_adj", [P, GB, N])
        q_hi = sb("q_hi", [P, NC, GB * N], F32R)
        q_lo = sb("q_lo", [P, NC, GB * N], F32R)
        k_parts = sb("k_parts", [P, 2, GB * N], F32R)
        k_blocks = [sb(f"k_blocks{c}", [P, 2, GB, HC, N], F32R) for c in range(NC)]
        v = sb("v", [P, GB, HID])

        neg_logits = sb("neg_logits", [P, A_RING, HC, N])
        probs = sb("probs", [P, E_RING, HC, N])
        probs_T = sb("probs_T", [P, PS_RING, HC, N])
        neg_max = sb("neg_max", [P, E_RING, HC])
        abs_max = sb("abs_max", [P, E_RING, HC])
        exp_sum = sb("exp_sum", [P, E_RING, HC])
        inv_sum = sb("inv_sum", [P, E_RING, HC])
        row_scale = sb("row_scale", [P, E_RING, HC])
        oT_hi = sb("oT_hi", [P, NC, GB * N], F32R)
        oT_lo = sb("oT_lo", [P, NC, GB * N], F32R)

        x_rows = sb("x_rows", [P, GB, HID])
        y = sb("y", [P, GB, HID])
        stats = sb("stats", [P, GB, 6])
        mean_var = sb("mean_var", [P, GB, 2])
        var_eps = sb("var_eps", [P, GB])
        inv_std = sb("inv_std", [P, GB])

        ps_scores = [psum(f"ps_scores{i}", [P, HC * N]) for i in range(2)]
        ps_probsT = [psum(f"ps_probsT{i}", [P, HC * N]) for i in range(2)]
        ps_oT = [psum(f"ps_oT{i}", [P, HC * N]) for i in range(2)]
        ps_proj = [psum(f"ps_proj{i}", [P, 512]) for i in range(2)]

        w_loaded = [sem(f"w_loaded_{w}") for w in "kqvo"]
        rows_loaded = sem("rows_loaded")
        w_split_hi = sem("w_split_hi")
        w_split_lo = sem("w_split_lo")
        wq_scaled = sem("wq_scaled")
        consts_ready = sem("consts_ready")
        ident_zeroed = sem("ident_zeroed")
        blocks_zeroed = sem("blocks_zeroed")
        xT_loaded = sem("xT_loaded")
        x_loaded = sem("x_loaded")
        adj_loaded = sem("adj_loaded")
        k_block_moved = [sem(f"k_block_moved{c}") for c in range(NC)]
        stored = sem("stored")
        xT_hi_done = sem("xT_hi_done")
        xT_lo_done = sem("xT_lo_done")
        neg_adj_done = sem("neg_adj_done")
        bo_added = sem("bo_added")
        qk_product = sem("qk_product")
        qk_hi_done = sem("qk_hi_done")
        qk_lo_done = sem("qk_lo_done")
        v_product = sem("v_product")
        v_done = sem("v_done")
        scores_done = sem("scores_done")
        logits_done = sem("logits_done")
        abs_done = sem("abs_done")
        exp_done = sem("exp_done")
        inv_done = sem("inv_done")
        row_scale_done = sem("row_scale_done")
        probs_scaled = sem("probs_scaled")
        transposed = sem("transposed")
        probs_T_done = sem("probs_T_done")
        values_done = sem("values_done")
        oT_hi_done = sem("oT_hi_done")
        oT_lo_done = sem("oT_lo_done")
        out_product = sem("out_product")
        y_done = sem("y_done")
        stats_done = sem("stats_done")
        mean_done = sem("mean_done")
        var_eps_done = sem("var_eps_done")
        inv_std_done = sem("inv_std_done")
        normed = sem("normed")

        def at(g, a_group, i):
            return g * a_group + (i + 1)

        def unit(g, u, prev, cur):
            if u >= UNITS:
                return None
            if u < 0:
                return (g - 1, u + UNITS) if prev else None
            return (g, u) if cur else None

        def bodies(engine, body):
            body(-1, prev=False, cur=False, nxt=True)
            body(0, prev=False, cur=True, nxt=True)
            with engine.Fori(1, GROUPS - 1) as g:
                body(g, prev=True, cur=True, nxt=True)
            body(GROUPS - 1, prev=True, cur=True, nxt=False)
            body(GROUPS, prev=True, cur=False, nxt=False)

        def two_units(t, u):
            b = u % GB - 1
            return t[:, b * N:(b + 2) * N]

        block = ctx.enter_context(nc.Block())

        @block.sync
        def _(sp):
            def load_xT(g):
                sp.dma_start(xT_raw[:], xT[bass.ds(g, 1)].rearrange("o p c n -> (o p) c n")).then_inc(xT_loaded, 16)

            def load_adj(g):
                sp.dma_start(adj_raw[:], adj[bass.ds(g * GB, GB)].rearrange("b n m -> n b m")).then_inc(adj_loaded, 16)

            def load_x(g):
                sp.dma_start(x_rows[:], x[bass.ds(g * GB, GB)].rearrange("b n d -> n b d")).then_inc(x_loaded, 16)

            def move_k(g, c):
                sp.wait_ge(qk_hi_done, at(g, 2 * NC, 2 * c))
                sp.wait_ge(qk_lo_done, at(g, 2 * NC, 2 * c))
                for h in range(HC):
                    rows = slice(h * HD, (h + 1) * HD)
                    sp.dma_start(k_blocks[c][rows].bitcast(F32).rearrange("p s b h m -> p (s b) h m")[:, :, h, :],
                                 k_parts[rows].bitcast(F32).rearrange("p s (b m) -> p (s b) m", b=GB)).then_inc(k_block_moved[c], 16)

            w_dram = {"k": wkT, "q": wqT, "v": wvT, "o": woT}
            for i, w in enumerate("kq"):
                sp.dma_start(w_raw[:, i], w_dram[w].rearrange("(c p) n -> p c n", p=P)).then_inc(w_loaded[i], 16)
                if i == 0:
                    load_xT(0)
            load_adj(0)
            sp.dma_start(bv_rows[:], bv.partition_broadcast(P)).then_inc(rows_loaded, 16)
            sp.dma_start(bo_rows[:], bo.partition_broadcast(P)).then_inc(rows_loaded, 16)
            for i, w in ((2, "v"), (3, "o")):
                sp.wait_ge(w_split_lo, i - 1)
                sp.dma_start(w_raw[:, i % 2], w_dram[w].rearrange("(c p) n -> p c n", p=P)).then_inc(w_loaded[i], 16)
            sp.wait_ge(blocks_zeroed, NC)

            def body(g, prev, cur, nxt):
                if nxt and cur:
                    sp.wait_ge(xT_hi_done, at(g, NC, NC - 1))
                    sp.wait_ge(xT_lo_done, at(g, NC, NC - 1))
                    load_xT(g + 1)
                    sp.wait_ge(neg_adj_done, at(g, GB, GB - 1))
                    load_adj(g + 1)
                if cur:
                    move_k(g, 2)
                    if prev:
                        sp.wait_ge(y_done, at(g - 1, GB, GB - 1))
                    load_x(g)
                if nxt:
                    move_k(g + 1, 0)
                if prev:
                    for b in range(GB):
                        sp.wait_ge(normed, at(g - 1, GB, b))
                        sp.dma_start(out[bass.ds((g - 1) * GB + b, 1)].rearrange("o n d -> (o n) d"),
                                     y[:, b]).then_inc(stored, 16)
                if nxt:
                    move_k(g + 1, 1)

            bodies(sp, body)
            sp.wait_ge(stored, 16 * GRAPHS)

        @block.gpsimd
        def _(pool):
            nc.gpsimd.memset(ident[:], 0.0).then_inc(ident_zeroed, 1)
            nc.gpsimd.memset(zeros[:], 0.0).then_inc(consts_ready, 1)
            nc.gpsimd.memset(neg_half[:], -0.5).then_inc(consts_ready, 1)
            pool.wait_ge(ident_zeroed, 1)
            nc.gpsimd.affine_select(out=ident[:], in_=ident[:], compare_op=ALU.not_equal, fill=1.0, base=0,
                                    pattern=[[-1, P]], channel_multiplier=1).then_inc(consts_ready, 1)
            for c in range(NC):
                nc.gpsimd.memset(k_blocks[c][:].rearrange("p s b h m -> p (s b h m)").bitcast(F32), 0.0) \
                    .then_inc(blocks_zeroed, 1)
            pool.wait_ge(consts_ready, 3)
            pool.wait_ge(adj_loaded, 16)
            for b in range(GB):
                nc.gpsimd.tensor_tensor(neg_adj[:, b], zeros[:], adj_raw[:, b], ALU.subtract).then_inc(neg_adj_done, 1)
            pool.wait_ge(rows_loaded, 32)

            def body(g, prev, cur, nxt):
                for s in range(UNITS):
                    for kc in {6: (0, 1), 7: (2,)}.get(s, ()) if nxt else ():
                        pool.wait_ge(xT_hi_done, at(g + 1, NC, kc))
                        nc.gpsimd.tensor_tensor(xT_lo[:, kc], xT_raw[:, kc], xT_hi[:, kc].bitcast(F32),
                                                ALU.subtract).then_inc(xT_lo_done, 1)
                    if prev and s < GB:
                        if s == 0:
                            pool.wait_ge(x_loaded, g * 16)
                        nc.gpsimd.tensor_tensor(x_rows[:, s], x_rows[:, s], bo_rows[:], ALU.add).then_inc(bo_added, 1)
                    if nxt and cur and s >= UNITS - GB:
                        b = s - (UNITS - GB)
                        if b == 0:
                            pool.wait_ge(adj_loaded, (g + 2) * 16)
                        pool.wait_ge(logits_done, at(g, UNITS, s))
                        nc.gpsimd.tensor_tensor(neg_adj[:, b], zeros[:], adj_raw[:, b], ALU.subtract) \
                            .then_inc(neg_adj_done, 1)
                    if prev and s == 8:
                        pool.wait_ge(var_eps_done, at(g - 1, 1, 0))
                        nc.gpsimd.tensor_tensor(inv_std[:], var_eps[:], neg_half[:], ALU.pow).then_inc(inv_std_done, 1)
                    if cur:
                        pool.wait_ge(row_scale_done, at(g, UNITS, s))
                        e = probs[:, s % E_RING]
                        nc.gpsimd.tensor_tensor(e, e, row_scale[:, s % E_RING].unsqueeze(2).to_broadcast([P, HC, N]),
                                                ALU.mult).then_inc(probs_scaled, 1)

            bodies(pool, body)

        @block.scalar
        def _(act):
            def exp_unit(g, u):
                act.wait_ge(logits_done, at(g, UNITS, u))
                r = u % E_RING
                for h in range(HC):
                    last = nc.scalar.activation(probs[:, r, h], neg_logits[:, u % A_RING, h], ACT.Exp, scale=-1.0,
                                                bias=neg_max[:, r, h:h + 1], accum_out=exp_sum[:, r, h:h + 1])
                last.then_inc(exp_done, 1)

            def qk_hi(g, c, is_q, bank):
                act.wait_ge(qk_product, at(g, 2 * NC, 2 * c + is_q))
                if not is_q:
                    if c > 0:
                        act.wait_ge(k_block_moved[c - 1], (g + 1) * 16 * HC)
                    else:
                        if isinstance(g, int) and g == 0:
                            pass
                        else:
                            act.wait_ge(k_block_moved[NC - 1], g * 16 * HC)
                dst = q_hi[:, c] if is_q else k_parts[:, 0]
                nc.scalar.copy(dst, ps_proj[bank][:]).then_inc(qk_hi_done, 1)

            def body(g, prev, cur, nxt):
                for s in range(UNITS):
                    if (s - O_LAG) % 2 == 1 and (w := unit(g, s - O_LAG, prev, cur)):
                        gw, u = w
                        c = u // GB
                        act.wait_ge(values_done, at(gw, UNITS, u))
                        if c == 0 and not (gw is g and not prev):
                            act.wait_ge(out_product, at(gw - 1, GB, u % GB))
                        nc.scalar.copy(two_units(oT_hi[:, c], u), two_units(ps_oT[(u // 2) % 2], 2 * ((u // 2) % 2) + 1)) \
                            .then_inc(oT_hi_done, 1)
                    if w := unit(g, s - T_LAG, prev, cur):
                        gw, u = w
                        act.wait_ge(transposed, at(gw, UNITS, u))
                        if u >= PS_RING or not (gw is g and not prev):
                            act.wait_ge(values_done, at(gw, UNITS, u - PS_RING))
                        nc.scalar.copy(probs_T[:, u % PS_RING].rearrange("p h n -> p (h n)"),
                                       ps_probsT[u % 2][:]).then_inc(probs_T_done, 1)
                    if nxt and s >= 9:
                        qk_hi(g + 1, (s - 9) // 2, (s - 9) % 2, (s - 9) % 2)
                    if cur and s == 0:
                        qk_hi(g, 1, 1, 1)
                    if cur:
                        if s >= E_RING or prev:
                            act.wait_ge(transposed, at(g, UNITS, s - E_RING))
                        exp_unit(g, s)
                    if cur and s in (4, 5):
                        qk_hi(g, 2, s - 4, 0)

            bodies(act, body)

        @block.vector
        def _(dve):
            for i, w in enumerate("kqvo"):
                raw = w_raw[:, i % 2]
                dve.wait_ge(w_loaded[i], 16)
                if w == "q":
                    nc.vector.tensor_scalar(raw, raw, -SCALE, None, ALU.mult).then_inc(wq_scaled, 1)
                    dve.wait_ge(wq_scaled, 1)
                nc.vector.tensor_copy(w_hi[w][:], raw).then_inc(w_split_hi, 1)
                dve.wait_ge(w_split_hi, i + 1)
                nc.vector.tensor_tensor(w_lo[w][:], raw, w_hi[w][:].bitcast(F32), ALU.subtract).then_inc(w_split_lo, 1)
                if i == 1:
                    dve.wait_ge(xT_loaded, 16)
                    for kc in range(NC):
                        nc.vector.tensor_copy(xT_hi[:, kc], xT_raw[:, kc]).then_inc(xT_hi_done, 1)

            def logits_waits(g, u):
                dve.wait_ge(scores_done, at(g, UNITS, u))
                if u < GB:
                    dve.wait_ge(neg_adj_done, at(g, GB, u))

            def minus_logits(u):
                b = u % GB
                for h in range(HC):
                    last = nc.vector.tensor_tensor_reduce(
                        out=neg_logits[:, u % A_RING, h], in0=ps_scores[u % 2][:, h * N:(h + 1) * N],
                        in1=neg_adj[:, b], scale=1.0, scalar=FLOAT_MAX, op0=ALU.add, op1=ALU.min,
                        accum_out=neg_max[:, u % E_RING, h:h + 1])
                last.then_inc(logits_done, 1)

            def qk_lo(g, c, is_q, bank):
                dve.wait_ge(qk_hi_done, at(g, 2 * NC, 2 * c + is_q))
                hi, lo = (q_hi[:, c], q_lo[:, c]) if is_q else (k_parts[:, 0], k_parts[:, 1])
                nc.vector.tensor_tensor(lo, ps_proj[bank][:], hi.bitcast(F32), ALU.subtract).then_inc(qk_lo_done, 1)

            def residual(g, b, bank, later):
                dve.wait_ge(out_product, at(g, GB, b))
                dve.wait_ge(bo_added, at(g, GB, b))
                if b == 0 and later:
                    dve.wait_ge(stored, g * GB * 16)
                nc.vector.tensor_tensor(y[:, b], ps_proj[bank][:, 0:HID], x_rows[:, b], ALU.add).then_inc(y_done, 1)
                dve.wait_ge(y_done, at(g, GB, b))
                nc.vector.bn_stats(stats[:, b], y[:, b]).then_inc(stats_done, 1)
                dve.wait_ge(w_split_lo, 4)
                dve.wait_ge(stats_done, at(g, GB, b))
                nc.vector.bn_aggr(mean_var[:, b], stats[:, b]).then_inc(mean_done, 1)

            def body(g, prev, cur, nxt):
                for s in range(UNITS):
                    if (s - O_LAG) % 2 == 1 and (w := unit(g, s - O_LAG, prev, cur)):
                        gw, u = w
                        c = u // GB
                        dve.wait_ge(oT_hi_done, at(gw, UNITS // 2, u // 2))
                        nc.vector.tensor_tensor(two_units(oT_lo[:, c], u),
                                                two_units(ps_oT[(u // 2) % 2], 2 * ((u // 2) % 2) + 1),
                                                two_units(oT_hi[:, c], u).bitcast(F32), ALU.subtract).then_inc(oT_lo_done, 1)
                    if cur:
                        logits_waits(g, s)
                    w = unit(g, s - 1, prev, cur)
                    if w:
                        gw, u = w
                        r = u % E_RING
                        dve.wait_ge(exp_done, at(gw, UNITS, u))
                        nc.vector.reciprocal(inv_sum[:, r], exp_sum[:, r]).then_inc(inv_done, 1)
                    if cur:
                        minus_logits(s)
                    if w:
                        dve.wait_ge(inv_done, at(gw, UNITS, u))
                        dve.wait_ge(abs_done, at(gw, UNITS, u))
                        nc.vector.scalar_tensor_tensor(out=row_scale[:, r], in0=abs_max[:, r], scalar=0.0,
                                                       in1=inv_sum[:, r], op0=ALU.is_gt, op1=ALU.mult) \
                            .then_inc(row_scale_done, 1)
                    if cur and s == 0:
                        qk_lo(g, 1, 1, 1)
                    if cur and 1 <= s <= GB:
                        b = s - 1
                        dve.wait_ge(v_product, at(g, GB, b))
                        if b == 0 and not prev:
                            dve.wait_ge(rows_loaded, 32)
                        if prev:
                            dve.wait_ge(values_done, at(g - 1, UNITS, UNITS - GB + b))
                        nc.vector.tensor_tensor(v[:, b], ps_proj[b % 2][:, 0:HID], bv_rows[:], ALU.add).then_inc(v_done, 1)
                    if prev and 5 <= s < 5 + GB:
                        b = s - 5
                        residual(g - 1, b, OUT_BANK[b], later=not (isinstance(g, int) and g == 1))
                    if prev and s == 8:
                        dve.wait_ge(mean_done, at(g - 1, GB, GB - 1))
                        nc.vector.tensor_scalar(var_eps[:], mean_var[:, :, 1], EPS, None, ALU.add).then_inc(var_eps_done, 1)
                    if nxt and s >= 9:
                        qk_lo(g + 1, (s - 9) // 2, (s - 9) % 2, (s - 9) % 2)
                    if cur:
                        dve.wait_ge(logits_done, at(g, UNITS, s))
                        nc.vector.tensor_reduce(abs_max[:, s % E_RING], neg_logits[:, s % A_RING], AX_X, ALU.max,
                                                apply_absolute_value=True).then_inc(abs_done, 1)
                    if cur and s in (4, 5):
                        qk_lo(g, 2, s - 4, 0)
                    if nxt and s == 6 and cur:
                        dve.wait_ge(xT_loaded, (g + 2) * 16)
                        dve.wait_ge(qk_product, at(g, 2 * NC, 2 * NC - 1))
                        for kc in range(NC):
                            nc.vector.tensor_copy(xT_hi[:, kc], xT_raw[:, kc]).then_inc(xT_hi_done, 1)
                    for b in {9: (0,), 10: (1, 2), 11: (3,)}.get(s, ()) if prev else ():
                        dve.wait_ge(inv_std_done, at(g - 1, 1, 0))
                        nc.vector.tensor_scalar(y[:, b], y[:, b], mean_var[:, b, 0:1], inv_std[:, b:b + 1],
                                                ALU.subtract, ALU.mult).then_inc(normed, 1)

            bodies(dve, body)

        @block.tensor
        def _(pe):
            def three_passes(ps, stationary, moving, lo_ready=None):
                (s_hi, s_lo), (m_hi, m_lo) = stationary, moving
                pairs = [(s_hi, m_hi), (s_lo, m_hi), (s_hi, m_lo)]
                for n, (a, b) in enumerate(pairs):
                    if n == 2 and lo_ready:
                        pe.wait_ge(*lo_ready)
                    for kc in range(NC):
                        last = pe.matmul(ps, a(kc), b(kc), start=(n == 0 and kc == 0),
                                         stop=(n == 2 and kc == NC - 1))
                return last

            def project_qk(g, c, is_q, bank, first=False):
                w = "q" if is_q else "k"
                cols = slice(c * P, (c + 1) * P)
                three_passes(ps_proj[bank][:],
                             (lambda kc: w_hi[w][:, kc, cols], lambda kc: w_lo[w][:, kc, cols]),
                             (lambda kc: xT_hi[:, kc], lambda kc: xT_lo[:, kc]),
                             lo_ready=(xT_lo_done, at(g, NC, NC - 1)) if first else None).then_inc(qk_product, 1)

            def project_v(g, b):
                nodes = slice(b * N, (b + 1) * N)
                three_passes(ps_proj[b % 2][:, 0:HID],
                             (lambda kc: xT_hi[:, kc, nodes], lambda kc: xT_lo[:, kc, nodes]),
                             (lambda kc: w_hi["v"][:, kc], lambda kc: w_lo["v"][:, kc])).then_inc(v_product, 1)

            def project_out(g, b, bank):
                pe.wait_ge(oT_lo_done, at(g, UNITS // 2, UNITS // 2 - 2 + b // 2))
                nodes = slice(b * N, (b + 1) * N)
                three_passes(ps_proj[bank][:, 0:HID],
                             (lambda kc: oT_hi[:, kc, nodes], lambda kc: oT_lo[:, kc, nodes]),
                             (lambda kc: w_hi["o"][:, kc], lambda kc: w_lo["o"][:, kc])).then_inc(out_product, 1)

            def scores(g, u, prev):
                c, b = divmod(u, GB)
                if b == 0:
                    pe.wait_ge(k_block_moved[c], (g + 1) * 16 * HC)
                    pe.wait_ge(qk_lo_done, at(g, 2 * NC, 2 * c + 1))
                if u >= 2 or prev:
                    pe.wait_ge(logits_done, at(g, UNITS, u - 2))
                nodes = slice(b * N, (b + 1) * N)
                for n, (q, part) in enumerate(((q_hi, 0), (q_lo, 0), (q_hi, 1))):
                    last = pe.matmul(ps_scores[u % 2][:], q[:, c, nodes],
                                     k_blocks[c][:, part, b].rearrange("p h m -> p (h m)"),
                                     start=(n == 0), stop=(n == 2))
                last.then_inc(scores_done, 1)

            def transposes(g, u, first):
                pe.wait_ge(probs_scaled, at(g, UNITS, u))
                if not first:
                    pe.wait_ge(probs_T_done, at(g, UNITS, u - 2))
                for h in range(HC):
                    last = pe.transpose(ps_probsT[u % 2][:, h * N:(h + 1) * N], probs[:, u % E_RING, h], ident[:])
                last.then_inc(transposed, 1)

            def values(g, u, first):
                c, b = divmod(u, GB)
                pe.wait_ge(probs_T_done, at(g, UNITS, u))
                if c == 0:
                    pe.wait_ge(v_done, at(g, GB, b))
                half = (u // 2) % 2
                if u % 2 == 0 and not first:
                    pe.wait_ge(oT_lo_done, at(g, UNITS // 2, u // 2 - 2))
                col = (2 * half + u % 2) * N
                for h in range(HC):
                    ch = (c * HC + h) * HD
                    last = pe.matmul(ps_oT[half][h * HD:(h + 1) * HD, col:col + N], v[:, b, ch:ch + HD],
                                     probs_T[:, u % PS_RING, h], start=True, stop=True)
                last.then_inc(values_done, 1)

            def body(g, prev, cur, nxt):
                for s in range(UNITS):
                    if cur:
                        scores(g, s, prev)
                    if w := unit(g, s - T_LAG, prev, cur):
                        transposes(*w, first=w[0] is g and not prev and w[1] < 2)
                    if w := unit(g, s - PV_LAG, prev, cur):
                        values(*w, first=w[0] is g and not prev and w[1] < 4)
                    if cur and s == 0:
                        pe.wait_ge(w_split_lo, 4)
                    if cur and s < GB:
                        if s < 2:
                            pe.wait_ge(qk_lo_done, at(g, 2 * NC, 2 + s))
                        else:
                            pe.wait_ge(v_done, at(g, GB, s - 2))
                        project_v(g, s)
                    if cur and s == 4:
                        pe.wait_ge(v_done, at(g, GB, 2))
                        project_qk(g, 2, 0, 0)
                    if prev and s == 4:
                        if cur:
                            pe.wait_ge(v_done, at(g, GB, 3))
                        else:
                            pe.wait_ge(y_done, at(g - 2, GB, 3))
                        project_out(g - 1, 0, 1)
                    if cur and s == 5:
                        pe.wait_ge(qk_lo_done, at(g, 2 * NC, 4))
                        project_qk(g, 2, 1, 0)
                    if prev and s == 5:
                        pe.wait_ge(y_done, at(g - 1, GB, 0))
                        project_out(g - 1, 1, 1)
                    if prev and s == 6:
                        if cur:
                            pe.wait_ge(qk_lo_done, at(g, 2 * NC, 5))
                        else:
                            pe.wait_ge(y_done, at(g - 2, GB, 2))
                        project_out(g - 1, 2, 0)
                    if prev and s == 7:
                        pe.wait_ge(y_done, at(g - 1, GB, 1))
                        project_out(g - 1, 3, 1)
                    if nxt and s == 8:
                        pe.wait_ge(xT_hi_done, at(g + 1, NC, NC - 1))
                        if prev:
                            pe.wait_ge(y_done, at(g - 1, GB, 2))
                        elif cur:
                            pe.wait_ge(qk_lo_done, at(g, 2 * NC, 5))
                        else:
                            pe.wait_ge(w_split_lo, 2)
                        project_qk(g + 1, 0, 0, 0, first=True)
                    if nxt and s == 9:
                        if prev:
                            pe.wait_ge(y_done, at(g - 1, GB, 3))
                        elif cur:
                            pe.wait_ge(v_done, at(g, GB, 3))
                        project_qk(g + 1, 0, 1, 1)
                    if nxt and s >= 10:
                        pe.wait_ge(qk_lo_done, at(g + 1, 2 * NC, s - 10))
                        project_qk(g + 1, 1, s % 2, s % 2)

            pe.wait_ge(consts_ready, 3)
            bodies(pe, body)


def kernel(x, adj, L0_gnn_Wq, L0_gnn_Wk, L0_gnn_Wv, L0_gnn_bv, L0_gnn_Wo, L0_gnn_bo):
    import numpy as np
    import concourse.bacc as bacc
    from concourse.bass_utils import run_bass_kernel_spmd

    x = np.ascontiguousarray(x)
    graphs, n, hid = x.shape
    xT = x.reshape(graphs // GB, GB, n, hid // 128, 128).transpose(0, 4, 3, 1, 2)
    arrays = {
        "x": x,
        "xT": np.ascontiguousarray(xT).reshape(graphs // GB, 128, hid // 128, GB * n),
        "adj": np.ascontiguousarray(adj),
        "wqT": np.ascontiguousarray(np.asarray(L0_gnn_Wq).T),
        "wkT": np.ascontiguousarray(np.asarray(L0_gnn_Wk).T),
        "wvT": np.ascontiguousarray(np.asarray(L0_gnn_Wv).T),
        "woT": np.ascontiguousarray(np.asarray(L0_gnn_Wo).T),
        "bv": np.ascontiguousarray(L0_gnn_bv),
        "bo": np.ascontiguousarray(L0_gnn_bo),
    }
    nc = bacc.Bacc("TRN2", target_bir_lowering=False, num_devices=1)
    args = [nc.dram_tensor(f"in_{name}", a.shape, mybir.dt.from_np(a.dtype), kind="ExternalInput").ap()
            for name, a in arrays.items()]
    args.append(nc.dram_tensor("out", x.shape, F32, kind="ExternalOutput").ap())
    graph_attention(nc, *args)
    r = run_bass_kernel_spmd(nc, [{f"in_{name}": a for name, a in arrays.items()}], core_ids=[0])
    return r.results[0]["out"]
```

```python
from contextlib import ExitStack

import concourse.bass as bass
from concourse import mybir

F32 = mybir.dt.float32
F32R = mybir.dt.float32r
ALU = mybir.AluOpType
ACT = mybir.ActivationFunctionType
AX_X = mybir.AxisListType.X

HEADS = 12
EPS = 1e-5
FLOAT_MAX = 3.4028234e38
GB = 4


def graph_attention(nc, x, xT, adj, wqT, wkT, wvT, woT, bv, bo, out):
    GRAPHS, N, HID = x.shape
    P = 128
    HD = HID // HEADS
    HC = P // HD
    PAIRS = HC // 2
    NC = HID // P
    GROUPS = GRAPHS // GB
    UNITS = NC * GB
    SCALE = float(HID) ** -0.5
    K_MOVES, Q_MOVES = 2 * HC, HC
    A_RING, E_RING, PS_RING = 3, 6, 2
    T_LAG, PV_LAG, O_LAG = 3, 4, 5
    assert N == P and HC * N == 512 and GB * N == 512

    ctx = ExitStack()
    with ctx:
        def sb(name, shape, dt=F32):
            return ctx.enter_context(nc.sbuf_tensor(name, shape, dt))

        def psum(name, shape):
            return ctx.enter_context(nc.psum_tensor(name, shape, F32))

        def sem(name):
            return ctx.enter_context(nc.semaphore(name))

        w_raw = sb("w_raw", [P, 2, NC, HID])
        w_hi = {w: sb(f"w{w}_hi", [P, NC, HID], F32R) for w in "qkvo"}
        w_lo = {w: sb(f"w{w}_lo", [P, NC, HID], F32R) for w in "qkvo"}
        bv_rows = sb("bv_rows", [P, HID])
        bo_rows = sb("bo_rows", [P, HID])
        ident = sb("ident", [P, P])
        zeros = sb("zeros", [P, P])
        neg_half = sb("neg_half", [P, GB])

        xT_raw = sb("xT_raw", [P, NC, GB * N])
        xT_hi = sb("xT_hi", [P, NC, GB * N], F32R)
        xT_lo = sb("xT_lo", [P, NC, GB * N], F32R)
        adj_raw = sb("adj_raw", [P, GB, N])
        neg_adj = sb("neg_adj", [P, GB, N])
        q_parts = sb("q_parts", [P, 2, 2, GB * N], F32R)
        k_parts = sb("k_parts", [P, 2, 2, GB * N], F32R)
        q_stack = sb("q_stack", [P, NC, 2, PAIRS, GB * N], F32R)
        k_stack = [sb(f"k_stack{c}", [P, PAIRS, GB, 2, N], F32R) for c in range(NC)]
        v = sb("v", [P, GB, HID])

        neg_logits = sb("neg_logits", [P, A_RING, HC, N])
        probs = sb("probs", [P, E_RING, HC, N])
        probs_T = sb("probs_T", [P, PS_RING, HC, N])
        neg_max = sb("neg_max", [P, E_RING, HC])
        abs_max = sb("abs_max", [P, E_RING, HC])
        exp_sum = sb("exp_sum", [P, E_RING, HC])
        inv_sum = sb("inv_sum", [P, E_RING, HC])
        row_scale = sb("row_scale", [P, E_RING, HC])
        oT_hi = sb("oT_hi", [P, NC, GB * N], F32R)
        oT_lo = sb("oT_lo", [P, NC, GB * N], F32R)

        x_rows = sb("x_rows", [P, GB, HID])
        y = sb("y", [P, GB, HID])
        stats = sb("stats", [P, GB, 6])
        mean_var = sb("mean_var", [P, GB, 2])
        var_eps = sb("var_eps", [P, GB])
        inv_std = sb("inv_std", [P, GB])

        ps_scores = [psum(f"ps_scores{i}", [P, HC * N]) for i in range(2)]
        ps_probsT = [psum(f"ps_probsT{i}", [P, HC * N]) for i in range(2)]
        ps_oT = [psum(f"ps_oT{i}", [P, HC * N]) for i in range(2)]
        ps_proj = [psum(f"ps_proj{i}", [P, 512]) for i in range(2)]

        w_loaded = [sem(f"w_loaded_{w}") for w in "kqvo"]
        rows_loaded = sem("rows_loaded")
        w_split_hi = sem("w_split_hi")
        w_split_lo = sem("w_split_lo")
        wq_scaled = sem("wq_scaled")
        wq_hi_done = sem("wq_hi_done")
        consts_ready = sem("consts_ready")
        ident_zeroed = sem("ident_zeroed")
        stacks_zeroed = sem("stacks_zeroed")
        xT_loaded = sem("xT_loaded")
        x_loaded = sem("x_loaded")
        adj_loaded = sem("adj_loaded")
        k_moved = [sem(f"k_moved{c}") for c in range(NC)]
        q_moved = [sem(f"q_moved{c}") for c in range(NC)]
        stored = sem("stored")
        xT_hi_done = sem("xT_hi_done")
        xT_lo_done = sem("xT_lo_done")
        neg_adj_done = sem("neg_adj_done")
        bo_added = sem("bo_added")
        qk_product = sem("qk_product")
        qk_hi_done = sem("qk_hi_done")
        qk_lo_done = sem("qk_lo_done")
        v_product = sem("v_product")
        v_done = sem("v_done")
        scores_done = sem("scores_done")
        logits_done = sem("logits_done")
        abs_done = sem("abs_done")
        exp_done = sem("exp_done")
        inv_done = sem("inv_done")
        row_scale_done = sem("row_scale_done")
        probs_scaled = sem("probs_scaled")
        transposed = sem("transposed")
        probs_T_done = sem("probs_T_done")
        values_done = sem("values_done")
        oT_hi_done = sem("oT_hi_done")
        oT_lo_done = sem("oT_lo_done")
        out_product = sem("out_product")
        y_done = sem("y_done")
        stats_done = sem("stats_done")
        mean_done = sem("mean_done")
        var_eps_done = sem("var_eps_done")
        inv_std_done = sem("inv_std_done")
        last_var_eps_done = sem("last_var_eps_done")
        last_inv_std_done = sem("last_inv_std_done")
        normed = sem("normed")

        def at(g, a_group, i):
            return g * a_group + (i + 1)

        def unit(g, u, prev, cur):
            if u >= UNITS:
                return None
            if u < 0:
                return (g - 1, u + UNITS) if prev else None
            return (g, u) if cur else None

        def bodies(engine, body):
            body(-1, prev=False, cur=False, nxt=True)
            body(0, prev=False, cur=True, nxt=True)
            with engine.Fori(1, GROUPS - 1) as g:
                body(g, prev=True, cur=True, nxt=True)
            body(GROUPS - 1, prev=True, cur=True, nxt=False)
            body(GROUPS, prev=True, cur=False, nxt=False)

        def two_units(t, u):
            b = u % GB - 1
            return t[:, b * N:(b + 2) * N]

        block = ctx.enter_context(nc.Block())

        @block.sync
        def _(sp):
            def load_xT(g):
                sp.dma_start(xT_raw[:], xT[bass.ds(g, 1)].rearrange("o p c n -> (o p) c n")).then_inc(xT_loaded, 16)

            def load_adj(g):
                sp.dma_start(adj_raw[:], adj[bass.ds(g * GB, GB)].rearrange("b n m -> n b m")).then_inc(adj_loaded, 16)

            def load_x(g):
                sp.dma_start(x_rows[:], x[bass.ds(g * GB, GB)].rearrange("b n d -> n b d")).then_inc(x_loaded, 16)

            def move_k(g, c):
                for r, part_done in enumerate((qk_hi_done, qk_lo_done)):
                    sp.wait_ge(part_done, at(g, 2 * NC, 2 * c))
                    for h in range(HC):
                        pair, j = divmod(h, 2)
                        row = r * P // 2 + j * HD
                        src = k_parts[h * HD:(h + 1) * HD, c % 2, r].rearrange("p (b m) -> p b m", b=GB)
                        sp.dma_start(k_stack[c][row:row + HD, pair, :, j].bitcast(F32),
                                     src.bitcast(F32)).then_inc(k_moved[c], 16)

            def move_q(g, c):
                sp.wait_ge(qk_lo_done, at(g, 2 * NC, 2 * c + 1))
                half = P // 2
                for pair in range(PAIRS):
                    for r in range(2):
                        sp.dma_start(q_stack[r * half:(r + 1) * half, c, :, pair].bitcast(F32),
                                     q_parts[pair * half:(pair + 1) * half, c % 2].bitcast(F32)).then_inc(q_moved[c], 16)

            w_dram = {"k": wkT, "q": wqT, "v": wvT, "o": woT}
            for i, w in enumerate("kq"):
                sp.dma_start(w_raw[:, i], w_dram[w].rearrange("(c p) n -> p c n", p=P)).then_inc(w_loaded[i], 16)
                if i == 0:
                    load_xT(0)
            load_adj(0)
            sp.dma_start(bv_rows[:], bv.partition_broadcast(P)).then_inc(rows_loaded, 16)
            sp.dma_start(bo_rows[:], bo.partition_broadcast(P)).then_inc(rows_loaded, 16)
            for i, w in ((2, "v"), (3, "o")):
                sp.wait_ge(w_split_lo, i - 1)
                sp.dma_start(w_raw[:, i % 2], w_dram[w].rearrange("(c p) n -> p c n", p=P)).then_inc(w_loaded[i], 16)
            sp.wait_ge(stacks_zeroed, NC)

            def store(g):
                sp.wait_ge(normed, at(g, GB, GB - 1))
                sp.dma_start(out[bass.ds(g * GB, GB)].rearrange("b n d -> n b d"), y[:]).then_inc(stored, 16)

            def body(g, prev, cur, nxt):
                if nxt and cur:
                    sp.wait_ge(xT_hi_done, at(g, NC, NC - 1))
                    sp.wait_ge(xT_lo_done, at(g, NC, NC - 1))
                    load_xT(g + 1)
                    sp.wait_ge(neg_adj_done, at(g, GB, GB - 1))
                    load_adj(g + 1)
                if cur:
                    move_k(g, 2)
                    move_q(g, 2)
                    if prev:
                        sp.wait_ge(y_done, at(g - 1, GB, GB - 1))
                    load_x(g)
                if nxt:
                    for c in range(2):
                        move_k(g + 1, c)
                        move_q(g + 1, c)
                if prev and cur:
                    store(g - 1)
                if prev and not cur:
                    for b0 in (0, 2):
                        sp.wait_ge(normed, at(g - 1, GB, b0 + 1))
                        sp.dma_start(out[bass.ds((g - 1) * GB + b0, 2)].rearrange("b n d -> n b d"),
                                     y[:, b0:b0 + 2]).then_inc(stored, 16)

            bodies(sp, body)
            sp.wait_ge(stored, 16 * (GROUPS + 1))

        @block.gpsimd
        def _(pool):
            nc.gpsimd.memset(ident[:], 0.0).then_inc(ident_zeroed, 1)
            nc.gpsimd.memset(zeros[:], 0.0).then_inc(consts_ready, 1)
            nc.gpsimd.memset(neg_half[:], -0.5).then_inc(consts_ready, 1)
            pool.wait_ge(ident_zeroed, 1)
            nc.gpsimd.affine_select(out=ident[:], in_=ident[:], compare_op=ALU.not_equal, fill=1.0, base=0,
                                    pattern=[[-1, P]], channel_multiplier=1).then_inc(consts_ready, 1)
            for c in range(NC):
                nc.gpsimd.memset(k_stack[c][:].rearrange("p i b j m -> p (i b j m)").bitcast(F32), 0.0) \
                    .then_inc(stacks_zeroed, 1)
            pool.wait_ge(consts_ready, 3)
            pool.wait_ge(adj_loaded, 16)
            for b in range(GB):
                nc.gpsimd.tensor_tensor(neg_adj[:, b], zeros[:], adj_raw[:, b], ALU.subtract).then_inc(neg_adj_done, 1)
            pool.wait_ge(rows_loaded, 32)

            def body(g, prev, cur, nxt):
                for s in range(UNITS):
                    if nxt and cur and 4 <= s < 4 + NC:
                        kc = s - 4
                        pool.wait_ge(xT_hi_done, at(g + 1, NC, kc))
                        nc.gpsimd.tensor_tensor(xT_lo[:, kc], xT_raw[:, kc], xT_hi[:, kc].bitcast(F32),
                                                ALU.subtract).then_inc(xT_lo_done, 1)
                    if prev and s < GB:
                        if s == 0:
                            pool.wait_ge(x_loaded, g * 16)
                        nc.gpsimd.tensor_tensor(x_rows[:, s], x_rows[:, s], bo_rows[:], ALU.add).then_inc(bo_added, 1)
                    if nxt and cur and s >= UNITS - GB:
                        b = s - (UNITS - GB)
                        if b == 0:
                            pool.wait_ge(adj_loaded, (g + 2) * 16)
                        pool.wait_ge(logits_done, at(g, UNITS, s))
                        nc.gpsimd.tensor_tensor(neg_adj[:, b], zeros[:], adj_raw[:, b], ALU.subtract) \
                            .then_inc(neg_adj_done, 1)
                    if prev and cur and s == 8:
                        pool.wait_ge(var_eps_done, at(g - 1, 1, 0))
                        nc.gpsimd.tensor_tensor(inv_std[:], var_eps[:], neg_half[:], ALU.pow).then_inc(inv_std_done, 1)
                    if cur:
                        pool.wait_ge(row_scale_done, at(g, UNITS, s))
                        e = probs[:, s % E_RING]
                        nc.gpsimd.tensor_tensor(e, e, row_scale[:, s % E_RING].unsqueeze(2).to_broadcast([P, HC, N]),
                                                ALU.mult).then_inc(probs_scaled, 1)
                if prev and not cur:
                    for i in range(2):
                        pair = slice(2 * i, 2 * i + 2)
                        pool.wait_ge(last_var_eps_done, i + 1)
                        nc.gpsimd.tensor_tensor(inv_std[:, pair], var_eps[:, pair], neg_half[:, pair], ALU.pow) \
                            .then_inc(last_inv_std_done, 1)

            bodies(pool, body)

        @block.scalar
        def _(act):
            act.wait_ge(w_loaded[1], 16)
            nc.scalar.mul(w_raw[:, 1], w_raw[:, 1], -SCALE).then_inc(wq_scaled, 1)
            act.wait_ge(wq_scaled, 1)
            nc.scalar.copy(w_hi["q"][:], w_raw[:, 1]).then_inc(wq_hi_done, 1)

            def exp_unit(g, u):
                act.wait_ge(logits_done, at(g, UNITS, u))
                r = u % E_RING
                for h in range(HC):
                    last = nc.scalar.activation(probs[:, r, h], neg_logits[:, u % A_RING, h], ACT.Exp, scale=-1.0,
                                                bias=neg_max[:, r, h:h + 1], accum_out=exp_sum[:, r, h:h + 1])
                last.then_inc(exp_done, 1)

            def qk_hi(g, i):
                c, is_q = divmod(i, 2)
                act.wait_ge(qk_product, at(g, 2 * NC, i))
                moved, moves, parts = (q_moved, Q_MOVES, q_parts) if is_q else (k_moved, K_MOVES, k_parts)
                if c == 2:
                    act.wait_ge(moved[0], (g + 1) * 16 * moves)
                elif not (isinstance(g, int) and g == 0):
                    act.wait_ge(moved[2 if c == 0 else 1], g * 16 * moves)
                nc.scalar.copy(parts[:, c % 2, 0], ps_proj[i % 2][:]).then_inc(qk_hi_done, 1)

            def body(g, prev, cur, nxt):
                for s in range(UNITS):
                    if (s - O_LAG) % 2 == 1 and (w := unit(g, s - O_LAG, prev, cur)):
                        gw, u = w
                        c = u // GB
                        act.wait_ge(values_done, at(gw, UNITS, u))
                        if c == 0 and not (gw is g and not prev):
                            act.wait_ge(out_product, at(gw - 1, GB, u % GB))
                        nc.scalar.copy(two_units(oT_hi[:, c], u), two_units(ps_oT[(u // 2) % 2], 2 * ((u // 2) % 2) + 1)) \
                            .then_inc(oT_hi_done, 1)
                    if w := unit(g, s - T_LAG, prev, cur):
                        gw, u = w
                        act.wait_ge(transposed, at(gw, UNITS, u))
                        if u >= PS_RING or not (gw is g and not prev):
                            act.wait_ge(values_done, at(gw, UNITS, u - PS_RING))
                        nc.scalar.copy(probs_T[:, u % PS_RING].rearrange("p h n -> p (h n)"),
                                       ps_probsT[u % 2][:]).then_inc(probs_T_done, 1)
                    if nxt and s >= 8:
                        qk_hi(g + 1, s - 8)
                    if cur and s < 2:
                        qk_hi(g, s + 4)
                    if cur:
                        if s >= E_RING or prev:
                            act.wait_ge(transposed, at(g, UNITS, s - E_RING))
                        exp_unit(g, s)

            bodies(act, body)

        @block.vector
        def _(dve):
            def split_weight(i):
                w, raw = "kqvo"[i], w_raw[:, i % 2]
                if w == "q":
                    dve.wait_ge(wq_hi_done, 1)
                else:
                    dve.wait_ge(w_loaded[i], 16)
                    nc.vector.tensor_copy(w_hi[w][:], raw).then_inc(w_split_hi, 1)
                    dve.wait_ge(w_split_hi, {"k": 1, "v": 2, "o": 3}[w])
                nc.vector.tensor_tensor(w_lo[w][:], raw, w_hi[w][:].bitcast(F32), ALU.subtract).then_inc(w_split_lo, 1)

            split_weight(0)
            dve.wait_ge(xT_loaded, 16)
            for kc in range(NC):
                nc.vector.tensor_copy(xT_hi[:, kc], xT_raw[:, kc]).then_inc(xT_hi_done, 1)
            for kc in range(NC):
                dve.wait_ge(xT_hi_done, kc + 1)
                nc.vector.tensor_tensor(xT_lo[:, kc], xT_raw[:, kc], xT_hi[:, kc].bitcast(F32),
                                        ALU.subtract).then_inc(xT_lo_done, 1)
            split_weight(1)

            def logits_waits(g, u):
                dve.wait_ge(scores_done, at(g, UNITS, u))
                if u < GB:
                    dve.wait_ge(neg_adj_done, at(g, GB, u))

            def minus_logits(u):
                b = u % GB
                for h in range(HC):
                    last = nc.vector.tensor_tensor_reduce(
                        out=neg_logits[:, u % A_RING, h], in0=ps_scores[u % 2][:, h * N:(h + 1) * N],
                        in1=neg_adj[:, b], scale=1.0, scalar=FLOAT_MAX, op0=ALU.add, op1=ALU.min,
                        accum_out=neg_max[:, u % E_RING, h:h + 1])
                last.then_inc(logits_done, 1)

            def qk_lo(g, i):
                c, is_q = divmod(i, 2)
                dve.wait_ge(qk_hi_done, at(g, 2 * NC, i))
                parts = q_parts if is_q else k_parts
                hi, lo = parts[:, c % 2, 0], parts[:, c % 2, 1]
                nc.vector.tensor_tensor(lo, ps_proj[i % 2][:], hi.bitcast(F32), ALU.subtract).then_inc(qk_lo_done, 1)

            def v_copy(g, b, prev):
                dve.wait_ge(v_product, at(g, GB, b))
                if b == 0 and not prev:
                    dve.wait_ge(rows_loaded, 32)
                if prev:
                    dve.wait_ge(values_done, at(g - 1, UNITS, UNITS - GB + b))
                nc.vector.tensor_tensor(v[:, b], ps_proj[b % 2][:, 0:HID], bv_rows[:], ALU.add).then_inc(v_done, 1)

            def residual(g, b):
                dve.wait_ge(out_product, at(g, GB, b))
                dve.wait_ge(bo_added, at(g, GB, b))
                if b == 0 and not (isinstance(g, int) and g == 0):
                    dve.wait_ge(stored, g * 16)
                nc.vector.tensor_tensor(y[:, b], ps_proj[b % 2][:, 0:HID], x_rows[:, b], ALU.add).then_inc(y_done, 1)

            def statistics(g, b):
                dve.wait_ge(y_done, at(g, GB, b))
                nc.vector.bn_stats(stats[:, b], y[:, b]).then_inc(stats_done, 1)

            def mean_and_variance(g, b):
                dve.wait_ge(w_split_lo, 4)
                dve.wait_ge(stats_done, at(g, GB, b))
                nc.vector.bn_aggr(mean_var[:, b], stats[:, b]).then_inc(mean_done, 1)

            def var_plus_eps(g, b0, b1, done):
                dve.wait_ge(mean_done, at(g, GB, b1 - 1))
                nc.vector.tensor_scalar(var_eps[:, b0:b1], mean_var[:, b0:b1, 1], EPS, None, ALU.add).then_inc(done, 1)

            def normalise(g, b):
                nc.vector.tensor_scalar(y[:, b], y[:, b], mean_var[:, b, 0:1], inv_std[:, b:b + 1],
                                        ALU.subtract, ALU.mult).then_inc(normed, 1)

            def last_layer_norms(g):
                for b0 in (0, 2):
                    for b in (b0, b0 + 1):
                        residual(g, b)
                    for b in (b0, b0 + 1):
                        statistics(g, b)
                    for b in (b0, b0 + 1):
                        mean_and_variance(g, b)
                    var_plus_eps(g, b0, b0 + 2, last_var_eps_done)
                for b in range(GB):
                    if b % 2 == 0:
                        dve.wait_ge(last_inv_std_done, b // 2 + 1)
                    normalise(g, b)

            def body(g, prev, cur, nxt):
                for s in range(UNITS):
                    if (s - O_LAG) % 2 == 1 and (w := unit(g, s - O_LAG, prev, cur)):
                        gw, u = w
                        c = u // GB
                        dve.wait_ge(oT_hi_done, at(gw, UNITS // 2, u // 2))
                        nc.vector.tensor_tensor(two_units(oT_lo[:, c], u),
                                                two_units(ps_oT[(u // 2) % 2], 2 * ((u // 2) % 2) + 1),
                                                two_units(oT_hi[:, c], u).bitcast(F32), ALU.subtract).then_inc(oT_lo_done, 1)
                    if cur and s == 2:
                        v_copy(g, 0, prev)
                    if prev and cur and s == 5:
                        residual(g - 1, 0)
                    if cur:
                        logits_waits(g, s)
                    w = unit(g, s - 1, prev, cur)
                    if w:
                        gw, u = w
                        r = u % E_RING
                        dve.wait_ge(exp_done, at(gw, UNITS, u))
                        nc.vector.reciprocal(inv_sum[:, r], exp_sum[:, r]).then_inc(inv_done, 1)
                    if cur:
                        minus_logits(s)
                    if w:
                        dve.wait_ge(inv_done, at(gw, UNITS, u))
                        dve.wait_ge(abs_done, at(gw, UNITS, u))
                        nc.vector.scalar_tensor_tensor(out=row_scale[:, r], in0=abs_max[:, r], scalar=0.0,
                                                       in1=inv_sum[:, r], op0=ALU.is_gt, op1=ALU.mult) \
                            .then_inc(row_scale_done, 1)
                    if nxt and s >= 8:
                        qk_lo(g + 1, s - 8)
                    if s in (9, 10) and not cur and nxt:
                        split_weight(s - 7)
                    if cur and s < 2:
                        qk_lo(g, s + 4)
                    if cur and s in (3, 4):
                        v_copy(g, s - 1, prev)
                    if prev and cur and s in (6, 7):
                        residual(g - 1, s - 4)
                    if prev and cur and 5 <= s < 5 + GB:
                        statistics(g - 1, s - 5)
                    if cur:
                        dve.wait_ge(logits_done, at(g, UNITS, s))
                        nc.vector.tensor_reduce(abs_max[:, s % E_RING], neg_logits[:, s % A_RING], AX_X, ALU.max,
                                                apply_absolute_value=True).then_inc(abs_done, 1)
                    if cur and s == 2:
                        v_copy(g, 1, prev)
                    if prev and cur and s == 5:
                        residual(g - 1, 1)
                    if prev and cur and 5 <= s < 5 + GB:
                        mean_and_variance(g - 1, s - 5)
                    if prev and cur and s == 8:
                        var_plus_eps(g - 1, 0, GB, var_eps_done)
                    if nxt and s == 4 and cur:
                        dve.wait_ge(xT_loaded, (g + 2) * 16)
                        dve.wait_ge(v_product, at(g, GB, GB - 1))
                        for kc in range(NC):
                            nc.vector.tensor_copy(xT_hi[:, kc], xT_raw[:, kc]).then_inc(xT_hi_done, 1)
                    for b in {9: (0,), 10: (1, 2), 11: (3,)}.get(s, ()) if prev and cur else ():
                        dve.wait_ge(inv_std_done, at(g - 1, 1, 0))
                        normalise(g - 1, b)
                if not cur and prev:
                    last_layer_norms(g - 1)

            bodies(dve, body)

        @block.tensor
        def _(pe):
            def three_passes(ps, stationary, moving, lo_ready=None):
                (s_hi, s_lo), (m_hi, m_lo) = stationary, moving
                pairs = [(s_hi, m_hi), (s_lo, m_hi), (s_hi, m_lo)]
                for n, (a, b) in enumerate(pairs):
                    if n == 2 and lo_ready:
                        pe.wait_ge(*lo_ready)
                    for kc in range(NC):
                        last = pe.matmul(ps, a(kc), b(kc), start=(n == 0 and kc == 0),
                                         stop=(n == 2 and kc == NC - 1))
                return last

            def project_qk(g, i, first=False):
                c, is_q = divmod(i, 2)
                w = "q" if is_q else "k"
                cols = slice(c * P, (c + 1) * P)
                three_passes(ps_proj[i % 2][:],
                             (lambda kc: w_hi[w][:, kc, cols], lambda kc: w_lo[w][:, kc, cols]),
                             (lambda kc: xT_hi[:, kc], lambda kc: xT_lo[:, kc]),
                             lo_ready=(xT_lo_done, at(g, NC, NC - 1)) if first else None).then_inc(qk_product, 1)

            def project_v(g, b):
                nodes = slice(b * N, (b + 1) * N)
                three_passes(ps_proj[b % 2][:, 0:HID],
                             (lambda kc: xT_hi[:, kc, nodes], lambda kc: xT_lo[:, kc, nodes]),
                             (lambda kc: w_hi["v"][:, kc], lambda kc: w_lo["v"][:, kc])).then_inc(v_product, 1)

            def project_out(g, b):
                pe.wait_ge(oT_lo_done, at(g, UNITS // 2, UNITS // 2 - 2 + b // 2))
                nodes = slice(b * N, (b + 1) * N)
                three_passes(ps_proj[b % 2][:, 0:HID],
                             (lambda kc: oT_hi[:, kc, nodes], lambda kc: oT_lo[:, kc, nodes]),
                             (lambda kc: w_hi["o"][:, kc], lambda kc: w_lo["o"][:, kc])).then_inc(out_product, 1)

            def scores(g, u, prev):
                c, b = divmod(u, GB)
                if b == 0:
                    pe.wait_ge(k_moved[c], (g + 1) * 16 * K_MOVES)
                    pe.wait_ge(q_moved[c], (g + 1) * 16 * Q_MOVES)
                if u >= 2 or prev:
                    pe.wait_ge(logits_done, at(g, UNITS, u - 2))
                for pair in range(PAIRS):
                    cols = slice(pair * 2 * N, (pair + 1) * 2 * N)
                    for part in range(2):
                        last = pe.matmul(ps_scores[u % 2][:, cols], q_stack[:, c, part, pair, b * N:(b + 1) * N],
                                         k_stack[c][:, pair, b].rearrange("p j m -> p (j m)"),
                                         start=(part == 0), stop=(part == 1))
                last.then_inc(scores_done, 1)

            def transposes(g, u, first):
                pe.wait_ge(probs_scaled, at(g, UNITS, u))
                if not first:
                    pe.wait_ge(probs_T_done, at(g, UNITS, u - 2))
                for h in range(HC):
                    last = pe.transpose(ps_probsT[u % 2][:, h * N:(h + 1) * N], probs[:, u % E_RING, h], ident[:])
                last.then_inc(transposed, 1)

            def values(g, u, first):
                c, b = divmod(u, GB)
                pe.wait_ge(probs_T_done, at(g, UNITS, u))
                if c == 0:
                    pe.wait_ge(v_done, at(g, GB, b))
                half = (u // 2) % 2
                if u % 2 == 0 and not first:
                    pe.wait_ge(oT_lo_done, at(g, UNITS // 2, u // 2 - 2))
                col = (2 * half + u % 2) * N
                for h in range(HC):
                    ch = (c * HC + h) * HD
                    last = pe.matmul(ps_oT[half][h * HD:(h + 1) * HD, col:col + N], v[:, b, ch:ch + HD],
                                     probs_T[:, u % PS_RING, h], start=True, stop=True)
                last.then_inc(values_done, 1)

            OUT_SLOTS = {4: (0,), 5: (1, 2), 6: (3,)}
            LAST_OUT_SLOTS = {2: (0,), 3: (1,), 5: (2,), 6: (3,)}

            def body(g, prev, cur, nxt):
                for s in range(UNITS):
                    if cur:
                        scores(g, s, prev)
                    if w := unit(g, s - T_LAG, prev, cur):
                        transposes(*w, first=w[0] is g and not prev and w[1] < 2)
                    if w := unit(g, s - PV_LAG, prev, cur):
                        values(*w, first=w[0] is g and not prev and w[1] < 4)
                    if cur and s == 0:
                        pe.wait_ge(qk_lo_done, at(g, 2 * NC, 3))
                        project_qk(g, 5)
                    for b in {1: (0,), 2: (1, 2), 3: (3,)}.get(s, ()) if cur else ():
                        if b < 2:
                            pe.wait_ge(qk_lo_done, at(g, 2 * NC, 4 + b))
                        else:
                            pe.wait_ge(v_done, at(g, GB, b - 2))
                        if b == 0:
                            pe.wait_ge(w_split_lo, 3)
                        project_v(g, b)
                    for b in (OUT_SLOTS if cur else LAST_OUT_SLOTS).get(s, ()) if prev else ():
                        if b >= 2:
                            pe.wait_ge(y_done, at(g - 1, GB, b - 2))
                        elif cur:
                            pe.wait_ge(v_done, at(g, GB, b + 2))
                        else:
                            pe.wait_ge(y_done, at(g - 2, GB, b + 2))
                        if b == 0:
                            pe.wait_ge(w_split_lo, 4)
                        project_out(g - 1, b)
                    if nxt and s >= 7:
                        i = s - 7
                        if i >= 2:
                            pe.wait_ge(qk_lo_done, at(g + 1, 2 * NC, i - 2))
                        elif prev:
                            pe.wait_ge(y_done, at(g - 1, GB, i + 2))
                        elif cur:
                            pe.wait_ge(v_done, at(g, GB, i + 2))
                        else:
                            pe.wait_ge(w_split_lo, i + 1)
                        if i == 0:
                            pe.wait_ge(xT_hi_done, at(g + 1, NC, NC - 1))
                        project_qk(g + 1, i, first=(i == 0))

            pe.wait_ge(consts_ready, 3)
            bodies(pe, body)


def kernel(x, adj, L0_gnn_Wq, L0_gnn_Wk, L0_gnn_Wv, L0_gnn_bv, L0_gnn_Wo, L0_gnn_bo):
    import numpy as np
    import concourse.bacc as bacc
    from concourse.bass_utils import run_bass_kernel_spmd

    x = np.ascontiguousarray(x)
    graphs, n, hid = x.shape
    xT = x.reshape(graphs // GB, GB, n, hid // 128, 128).transpose(0, 4, 3, 1, 2)
    arrays = {
        "x": x,
        "xT": np.ascontiguousarray(xT).reshape(graphs // GB, 128, hid // 128, GB * n),
        "adj": np.ascontiguousarray(adj),
        "wqT": np.ascontiguousarray(np.asarray(L0_gnn_Wq).T),
        "wkT": np.ascontiguousarray(np.asarray(L0_gnn_Wk).T),
        "wvT": np.ascontiguousarray(np.asarray(L0_gnn_Wv).T),
        "woT": np.ascontiguousarray(np.asarray(L0_gnn_Wo).T),
        "bv": np.ascontiguousarray(L0_gnn_bv),
        "bo": np.ascontiguousarray(L0_gnn_bo),
    }
    nc = bacc.Bacc("TRN2", target_bir_lowering=False, num_devices=1)
    args = [nc.dram_tensor(f"in_{name}", a.shape, mybir.dt.from_np(a.dtype), kind="ExternalInput").ap()
            for name, a in arrays.items()]
    args.append(nc.dram_tensor("out", x.shape, F32, kind="ExternalOutput").ap())
    graph_attention(nc, *args)
    r = run_bass_kernel_spmd(nc, [{f"in_{name}": a for name, a in arrays.items()}], core_ids=[0])
    return r.results[0]["out"]
```

```python
from contextlib import ExitStack

import concourse.bass as bass
from concourse import mybir

F32 = mybir.dt.float32
F32R = mybir.dt.float32r
ALU = mybir.AluOpType
ACT = mybir.ActivationFunctionType
AX_X = mybir.AxisListType.X

HEADS = 12
EPS = 1e-5
FLOAT_MAX = 3.4028234e38
GB = 4


def graph_attention(nc, x, xT, adj, wqT, wkT, wvT, woT, bv, bo, out):
    GRAPHS, N, HID = x.shape
    P = 128
    HD = HID // HEADS
    HC = P // HD
    PAIRS = HC // 2
    NC = HID // P
    GROUPS = GRAPHS // GB
    UNITS = NC * GB
    SCALE = float(HID) ** -0.5
    K_MOVES, Q_MOVES = 2 * HC, HC
    A_RING, E_RING, PS_RING = 3, 6, 2
    T_LAG, PV_LAG, O_LAG = 3, 4, 5
    assert N == P and HC * N == 512 and GB * N == 512

    ctx = ExitStack()
    with ctx:
        def sb(name, shape, dt=F32):
            return ctx.enter_context(nc.sbuf_tensor(name, shape, dt))

        def psum(name, shape):
            return ctx.enter_context(nc.psum_tensor(name, shape, F32))

        def sem(name):
            return ctx.enter_context(nc.semaphore(name))

        w_raw = sb("w_raw", [P, 2, NC, HID])
        w_hi = {w: sb(f"w{w}_hi", [P, NC, HID], F32R) for w in "qkvo"}
        w_lo = {w: sb(f"w{w}_lo", [P, NC, HID], F32R) for w in "qkvo"}
        bv_rows = sb("bv_rows", [P, HID])
        bo_rows = sb("bo_rows", [P, HID])
        ident = sb("ident", [P, P])
        zeros = sb("zeros", [P, P])
        neg_half = sb("neg_half", [P, GB])

        xT_raw = sb("xT_raw", [P, NC, GB * N])
        xT_hi = sb("xT_hi", [P, NC, GB * N], F32R)
        xT_lo = sb("xT_lo", [P, NC, GB * N], F32R)
        adj_raw = sb("adj_raw", [P, GB, N])
        neg_adj = sb("neg_adj", [P, GB, N])
        q_parts = sb("q_parts", [P, 2, 2, GB * N], F32R)
        k_parts = sb("k_parts", [P, 2, 2, GB * N], F32R)
        q_stack = sb("q_stack", [P, NC, 2, PAIRS, GB * N], F32R)
        k_stack = [sb(f"k_stack{c}", [P, PAIRS, GB, 2, N], F32R) for c in range(NC)]
        v = sb("v", [P, GB, HID])

        neg_logits = sb("neg_logits", [P, A_RING, HC, N])
        probs = sb("probs", [P, E_RING, HC, N])
        probs_T = sb("probs_T", [P, PS_RING, HC, N])
        neg_max = sb("neg_max", [P, E_RING, HC])
        abs_max = sb("abs_max", [P, E_RING, HC])
        exp_sum = sb("exp_sum", [P, E_RING, HC])
        inv_sum = sb("inv_sum", [P, E_RING, HC])
        row_scale = sb("row_scale", [P, E_RING, HC])
        oT_hi = sb("oT_hi", [P, NC, GB * N], F32R)
        oT_lo = sb("oT_lo", [P, NC, GB * N], F32R)

        x_rows = sb("x_rows", [P, GB, HID])
        y = sb("y", [P, GB, HID])
        stats = sb("stats", [P, GB, 6])
        mean_var = sb("mean_var", [P, GB, 2])
        var_eps = sb("var_eps", [P, GB])
        inv_std = sb("inv_std", [P, GB])

        ps_scores = [psum(f"ps_scores{i}", [P, HC * N]) for i in range(2)]
        ps_probsT = [psum(f"ps_probsT{i}", [P, HC * N]) for i in range(2)]
        ps_oT = [psum(f"ps_oT{i}", [P, HC * N]) for i in range(2)]
        ps_proj = [psum(f"ps_proj{i}", [P, 512]) for i in range(2)]

        w_loaded = [sem(f"w_loaded_{w}") for w in "kqvo"]
        rows_loaded = sem("rows_loaded")
        w_split_hi = sem("w_split_hi")
        w_split_lo = sem("w_split_lo")
        wq_hi_done = sem("wq_hi_done")
        consts_ready = sem("consts_ready")
        ident_zeroed = sem("ident_zeroed")
        stacks_zeroed = sem("stacks_zeroed")
        xT_loaded = sem("xT_loaded")
        xT_chunk_loaded = [sem(f"xT_chunk_loaded{kc}") for kc in range(NC)]
        x_loaded = sem("x_loaded")
        adj_loaded = sem("adj_loaded")
        k_moved = [sem(f"k_moved{c}") for c in range(NC)]
        q_moved = [sem(f"q_moved{c}") for c in range(NC)]
        stored = sem("stored")
        xT_hi_done = sem("xT_hi_done")
        xT_lo_done = sem("xT_lo_done")
        neg_adj_done = sem("neg_adj_done")
        bo_added = sem("bo_added")
        qk_product = sem("qk_product")
        qk_hi_done = sem("qk_hi_done")
        qk_lo_done = sem("qk_lo_done")
        v_product = sem("v_product")
        v_done = sem("v_done")
        scores_done = sem("scores_done")
        logits_done = sem("logits_done")
        abs_done = sem("abs_done")
        exp_done = sem("exp_done")
        inv_done = sem("inv_done")
        row_scale_done = sem("row_scale_done")
        probs_scaled = sem("probs_scaled")
        transposed = sem("transposed")
        probs_T_done = sem("probs_T_done")
        values_done = sem("values_done")
        oT_hi_done = sem("oT_hi_done")
        oT_lo_done = sem("oT_lo_done")
        out_product = sem("out_product")
        y_done = sem("y_done")
        stats_done = sem("stats_done")
        mean_done = sem("mean_done")
        var_eps_done = sem("var_eps_done")
        inv_std_done = sem("inv_std_done")
        last_var_eps_done = sem("last_var_eps_done")
        last_inv_std_done = sem("last_inv_std_done")
        normed = sem("normed")

        def at(g, a_group, i):
            return g * a_group + (i + 1)

        def unit(g, u, prev, cur):
            if u >= UNITS:
                return None
            if u < 0:
                return (g - 1, u + UNITS) if prev else None
            return (g, u) if cur else None

        def bodies(engine, body):
            body(-1, prev=False, cur=False, nxt=True)
            body(0, prev=False, cur=True, nxt=True)
            with engine.Fori(1, GROUPS - 1) as g:
                body(g, prev=True, cur=True, nxt=True)
            body(GROUPS - 1, prev=True, cur=True, nxt=False)
            body(GROUPS, prev=True, cur=False, nxt=False)

        def two_units(t, u):
            b = u % GB - 1
            return t[:, b * N:(b + 2) * N]

        LAST_OUT_BANKS = ps_proj + ps_scores

        block = ctx.enter_context(nc.Block())

        @block.sync
        def _(sp):
            def load_xT(g):
                sp.dma_start(xT_raw[:], xT[bass.ds(g, 1)].rearrange("o p c n -> (o p) c n")).then_inc(xT_loaded, 16)

            def load_adj(g):
                sp.dma_start(adj_raw[:], adj[bass.ds(g * GB, GB)].rearrange("b n m -> n b m")).then_inc(adj_loaded, 16)

            def load_x(g):
                sp.dma_start(x_rows[:], x[bass.ds(g * GB, GB)].rearrange("b n d -> n b d")).then_inc(x_loaded, 16)

            def move_k(g, c):
                for r, part_done in enumerate((qk_hi_done, qk_lo_done)):
                    sp.wait_ge(part_done, at(g, 2 * NC, 2 * c))
                    for h in range(HC):
                        pair, j = divmod(h, 2)
                        row = r * P // 2 + j * HD
                        src = k_parts[h * HD:(h + 1) * HD, c % 2, r].rearrange("p (b m) -> p b m", b=GB)
                        sp.dma_start(k_stack[c][row:row + HD, pair, :, j].bitcast(F32),
                                     src.bitcast(F32)).then_inc(k_moved[c], 16)

            def move_q(g, c):
                sp.wait_ge(qk_lo_done, at(g, 2 * NC, 2 * c + 1))
                half = P // 2
                for pair in range(PAIRS):
                    for r in range(2):
                        sp.dma_start(q_stack[r * half:(r + 1) * half, c, :, pair].bitcast(F32),
                                     q_parts[pair * half:(pair + 1) * half, c % 2].bitcast(F32)).then_inc(q_moved[c], 16)

            w_dram = {"k": wkT, "q": wqT, "v": wvT, "o": woT}
            for i, w in enumerate("kq"):
                sp.dma_start(w_raw[:, i], w_dram[w].rearrange("(c p) n -> p c n", p=P)).then_inc(w_loaded[i], 16)
                if i == 0:
                    for kc in range(NC):
                        sp.dma_start(xT_raw[:, kc], xT[0:1, :, kc].rearrange("o p n -> (o p) n")) \
                            .then_inc(xT_chunk_loaded[kc], 16)
            load_adj(0)
            sp.dma_start(bv_rows[:], bv.partition_broadcast(P)).then_inc(rows_loaded, 16)
            sp.dma_start(bo_rows[:], bo.partition_broadcast(P)).then_inc(rows_loaded, 16)
            for i, w in ((2, "v"), (3, "o")):
                sp.wait_ge(w_split_lo, i - 1)
                sp.dma_start(w_raw[:, i % 2], w_dram[w].rearrange("(c p) n -> p c n", p=P)).then_inc(w_loaded[i], 16)
            sp.wait_ge(stacks_zeroed, NC)

            def store(g):
                sp.wait_ge(normed, at(g, GB, GB - 1))
                sp.dma_start(out[bass.ds(g * GB, GB)].rearrange("b n d -> n b d"), y[:]).then_inc(stored, 16)

            def next_xT(g):
                sp.wait_ge(xT_hi_done, at(g, NC, NC - 1))
                sp.wait_ge(xT_lo_done, at(g, NC, NC - 1))
                load_xT(g + 1)

            def body(g, prev, cur, nxt):
                if not cur and nxt:
                    next_xT(0)
                if nxt and cur:
                    if prev:
                        next_xT(g)
                    sp.wait_ge(neg_adj_done, at(g, GB, GB - 1))
                    load_adj(g + 1)
                if cur:
                    move_q(g, 2)
                    if prev:
                        sp.wait_ge(y_done, at(g - 1, GB, GB - 1))
                    load_x(g)
                if nxt:
                    for c in range(2):
                        move_k(g + 1, c)
                        move_q(g + 1, c)
                    move_k(g + 1, 2)
                if prev and cur:
                    store(g - 1)
                if prev and not cur:
                    for b0 in (0, 2):
                        sp.wait_ge(normed, at(g - 1, GB, b0 + 1))
                        sp.dma_start(out[bass.ds((g - 1) * GB + b0, 2)].rearrange("b n d -> n b d"),
                                     y[:, b0:b0 + 2]).then_inc(stored, 16)

            bodies(sp, body)
            sp.wait_ge(stored, 16 * (GROUPS + 1))

        @block.gpsimd
        def _(pool):
            nc.gpsimd.memset(ident[:], 0.0).then_inc(ident_zeroed, 1)
            nc.gpsimd.memset(zeros[:], 0.0).then_inc(consts_ready, 1)
            nc.gpsimd.memset(neg_half[:], -0.5).then_inc(consts_ready, 1)
            pool.wait_ge(ident_zeroed, 1)
            nc.gpsimd.affine_select(out=ident[:], in_=ident[:], compare_op=ALU.not_equal, fill=1.0, base=0,
                                    pattern=[[-1, P]], channel_multiplier=1).then_inc(consts_ready, 1)
            for c in range(NC):
                nc.gpsimd.memset(k_stack[c][:].rearrange("p i b j m -> p (i b j m)").bitcast(F32), 0.0) \
                    .then_inc(stacks_zeroed, 1)
            pool.wait_ge(consts_ready, 3)
            pool.wait_ge(adj_loaded, 16)
            for b in range(GB):
                nc.gpsimd.tensor_tensor(neg_adj[:, b], zeros[:], adj_raw[:, b], ALU.subtract).then_inc(neg_adj_done, 1)
            pool.wait_ge(rows_loaded, 32)

            def body(g, prev, cur, nxt):
                for s in range(UNITS):
                    for kc in {4: (0, 1), 5: (2,)}.get(s, ()) if nxt and prev else ():
                        pool.wait_ge(xT_hi_done, at(g + 1, NC, kc))
                        nc.gpsimd.tensor_tensor(xT_lo[:, kc], xT_raw[:, kc], xT_hi[:, kc].bitcast(F32),
                                                ALU.subtract).then_inc(xT_lo_done, 1)
                    if prev and s < GB:
                        if s == 0:
                            pool.wait_ge(x_loaded, g * 16)
                        nc.gpsimd.tensor_tensor(x_rows[:, s], x_rows[:, s], bo_rows[:], ALU.add).then_inc(bo_added, 1)
                    if nxt and cur and s >= UNITS - GB:
                        b = s - (UNITS - GB)
                        if b == 0:
                            pool.wait_ge(adj_loaded, (g + 2) * 16)
                        pool.wait_ge(logits_done, at(g, UNITS, s))
                        nc.gpsimd.tensor_tensor(neg_adj[:, b], zeros[:], adj_raw[:, b], ALU.subtract) \
                            .then_inc(neg_adj_done, 1)
                    if prev and cur and s == 8:
                        pool.wait_ge(var_eps_done, at(g - 1, 1, 0))
                        nc.gpsimd.tensor_tensor(inv_std[:], var_eps[:], neg_half[:], ALU.pow).then_inc(inv_std_done, 1)
                    if cur:
                        pool.wait_ge(row_scale_done, at(g, UNITS, s))
                        e = probs[:, s % E_RING]
                        nc.gpsimd.tensor_tensor(e, e, row_scale[:, s % E_RING].unsqueeze(2).to_broadcast([P, HC, N]),
                                                ALU.mult).then_inc(probs_scaled, 1)
                if prev and not cur:
                    for i in range(2):
                        pair = slice(2 * i, 2 * i + 2)
                        pool.wait_ge(last_var_eps_done, i + 1)
                        nc.gpsimd.tensor_tensor(inv_std[:, pair], var_eps[:, pair], neg_half[:, pair], ALU.pow) \
                            .then_inc(last_inv_std_done, 1)

            bodies(pool, body)

        @block.scalar
        def _(act):
            act.wait_ge(w_loaded[1], 16)
            nc.scalar.mul(w_hi["q"][:], w_raw[:, 1], -SCALE).then_inc(wq_hi_done, 1)

            def exp_unit(g, u):
                act.wait_ge(logits_done, at(g, UNITS, u))
                r = u % E_RING
                for h in range(HC):
                    last = nc.scalar.activation(probs[:, r, h], neg_logits[:, u % A_RING, h], ACT.Exp, scale=-1.0,
                                                bias=neg_max[:, r, h:h + 1], accum_out=exp_sum[:, r, h:h + 1])
                last.then_inc(exp_done, 1)

            def qk_hi(g, i):
                c, is_q = divmod(i, 2)
                act.wait_ge(qk_product, at(g, 2 * NC, i))
                moved, moves, parts = (q_moved, Q_MOVES, q_parts) if is_q else (k_moved, K_MOVES, k_parts)
                if c == 2:
                    act.wait_ge(moved[0], (g + 1) * 16 * moves)
                elif not (isinstance(g, int) and g == 0):
                    act.wait_ge(moved[2 if c == 0 else 1], g * 16 * moves)
                nc.scalar.copy(parts[:, c % 2, 0], ps_proj[i % 2][:]).then_inc(qk_hi_done, 1)

            def body(g, prev, cur, nxt):
                for s in range(UNITS):
                    if (s - O_LAG) % 2 == 1 and (w := unit(g, s - O_LAG, prev, cur)):
                        gw, u = w
                        c = u // GB
                        act.wait_ge(values_done, at(gw, UNITS, u))
                        if c == 0 and not (gw is g and not prev):
                            act.wait_ge(out_product, at(gw - 1, GB, u % GB))
                        nc.scalar.copy(two_units(oT_hi[:, c], u), two_units(ps_oT[(u // 2) % 2], 2 * ((u // 2) % 2) + 1)) \
                            .then_inc(oT_hi_done, 1)
                    if w := unit(g, s - T_LAG, prev, cur):
                        gw, u = w
                        act.wait_ge(transposed, at(gw, UNITS, u))
                        if u >= PS_RING or not (gw is g and not prev):
                            act.wait_ge(values_done, at(gw, UNITS, u - PS_RING))
                        nc.scalar.copy(probs_T[:, u % PS_RING].rearrange("p h n -> p (h n)"),
                                       ps_probsT[u % 2][:]).then_inc(probs_T_done, 1)
                    if nxt and s >= 7:
                        qk_hi(g + 1, s - 7)
                    if cur and s == 0:
                        qk_hi(g, 5)
                    if cur:
                        if s >= E_RING or prev:
                            act.wait_ge(transposed, at(g, UNITS, s - E_RING))
                        exp_unit(g, s)

            bodies(act, body)

        @block.vector
        def _(dve):
            def first_xT_hi(kc):
                dve.wait_ge(xT_chunk_loaded[kc], 16)
                nc.vector.tensor_copy(xT_hi[:, kc], xT_raw[:, kc]).then_inc(xT_hi_done, 1)

            def early_xT_lo(g):
                for kc in range(NC):
                    dve.wait_ge(xT_hi_done, at(g, NC, kc))
                    nc.vector.tensor_tensor(xT_lo[:, kc], xT_raw[:, kc], xT_hi[:, kc].bitcast(F32),
                                            ALU.subtract).then_inc(xT_lo_done, 1)

            def split_weight(i):
                w, raw = "kqvo"[i], w_raw[:, i % 2]
                if w == "q":
                    dve.wait_ge(wq_hi_done, 1)
                    nc.vector.scalar_tensor_tensor(out=w_lo[w][:], in0=raw, scalar=-SCALE, in1=w_hi[w][:].bitcast(F32),
                                                   op0=ALU.mult, op1=ALU.subtract).then_inc(w_split_lo, 1)
                    return
                dve.wait_ge(w_loaded[i], 16)
                nc.vector.tensor_copy(w_hi[w][:], raw).then_inc(w_split_hi, 1)
                dve.wait_ge(w_split_hi, {"k": 1, "v": 2, "o": 3}[w])
                if w == "k":
                    first_xT_hi(0)
                nc.vector.tensor_tensor(w_lo[w][:], raw, w_hi[w][:].bitcast(F32), ALU.subtract).then_inc(w_split_lo, 1)

            split_weight(0)
            for kc in range(1, NC):
                first_xT_hi(kc)
            early_xT_lo(0)
            split_weight(1)

            def logits_waits(g, u):
                dve.wait_ge(scores_done, at(g, UNITS, u))
                if u < GB:
                    dve.wait_ge(neg_adj_done, at(g, GB, u))

            def minus_logits(u):
                b = u % GB
                for h in range(HC):
                    last = nc.vector.tensor_tensor_reduce(
                        out=neg_logits[:, u % A_RING, h], in0=ps_scores[u % 2][:, h * N:(h + 1) * N],
                        in1=neg_adj[:, b], scale=1.0, scalar=FLOAT_MAX, op0=ALU.add, op1=ALU.min,
                        accum_out=neg_max[:, u % E_RING, h:h + 1])
                last.then_inc(logits_done, 1)

            def qk_lo(g, i):
                c, is_q = divmod(i, 2)
                dve.wait_ge(qk_hi_done, at(g, 2 * NC, i))
                parts = q_parts if is_q else k_parts
                hi, lo = parts[:, c % 2, 0], parts[:, c % 2, 1]
                nc.vector.tensor_tensor(lo, ps_proj[i % 2][:], hi.bitcast(F32), ALU.subtract).then_inc(qk_lo_done, 1)

            def v_copy(g, b, prev):
                dve.wait_ge(v_product, at(g, GB, b))
                if b == 0 and not prev:
                    dve.wait_ge(rows_loaded, 32)
                if prev:
                    dve.wait_ge(values_done, at(g - 1, UNITS, UNITS - GB + b))
                nc.vector.tensor_tensor(v[:, b], ps_proj[b % 2][:, 0:HID], bv_rows[:], ALU.add).then_inc(v_done, 1)

            def residual(g, b, bank=None):
                dve.wait_ge(out_product, at(g, GB, b))
                dve.wait_ge(bo_added, at(g, GB, b))
                if b == 0 and not (isinstance(g, int) and g == 0):
                    dve.wait_ge(stored, g * 16)
                nc.vector.tensor_tensor(y[:, b], (bank or ps_proj[b % 2])[:, 0:HID], x_rows[:, b], ALU.add).then_inc(y_done, 1)

            def statistics(g, b):
                dve.wait_ge(y_done, at(g, GB, b))
                nc.vector.bn_stats(stats[:, b], y[:, b]).then_inc(stats_done, 1)

            def mean_and_variance(g, b):
                dve.wait_ge(w_split_lo, 4)
                dve.wait_ge(stats_done, at(g, GB, b))
                nc.vector.bn_aggr(mean_var[:, b], stats[:, b]).then_inc(mean_done, 1)

            def var_plus_eps(g, b0, b1, done):
                dve.wait_ge(mean_done, at(g, GB, b1 - 1))
                nc.vector.tensor_scalar(var_eps[:, b0:b1], mean_var[:, b0:b1, 1], EPS, None, ALU.add).then_inc(done, 1)

            def normalise(g, b):
                nc.vector.tensor_scalar(y[:, b], y[:, b], mean_var[:, b, 0:1], inv_std[:, b:b + 1],
                                        ALU.subtract, ALU.mult).then_inc(normed, 1)

            def last_layer_norms(g):
                for b0 in (0, 2):
                    for b in (b0, b0 + 1):
                        residual(g, b, LAST_OUT_BANKS[b])
                    for b in (b0, b0 + 1):
                        statistics(g, b)
                    for b in (b0, b0 + 1):
                        mean_and_variance(g, b)
                    var_plus_eps(g, b0, b0 + 2, last_var_eps_done)
                for b in range(GB):
                    if b % 2 == 0:
                        dve.wait_ge(last_inv_std_done, b // 2 + 1)
                    normalise(g, b)

            def body(g, prev, cur, nxt):
                for s in range(UNITS):
                    if cur and s == 4:
                        v_copy(g, 3, prev)
                    if prev and cur and s in (5, 6):
                        residual(g - 1, 2 * (s - 5))
                    if cur:
                        logits_waits(g, s)
                    w = unit(g, s - 1, prev, cur)
                    if w:
                        gw, u = w
                        r = u % E_RING
                        dve.wait_ge(exp_done, at(gw, UNITS, u))
                        nc.vector.reciprocal(inv_sum[:, r], exp_sum[:, r]).then_inc(inv_done, 1)
                    if cur:
                        minus_logits(s)
                    if w:
                        dve.wait_ge(inv_done, at(gw, UNITS, u))
                        dve.wait_ge(abs_done, at(gw, UNITS, u))
                        nc.vector.scalar_tensor_tensor(out=row_scale[:, r], in0=abs_max[:, r], scalar=0.0,
                                                       in1=inv_sum[:, r], op0=ALU.is_gt, op1=ALU.mult) \
                            .then_inc(row_scale_done, 1)
                    if (s - O_LAG) % 2 == 1 and (w2 := unit(g, s - O_LAG, prev, cur)):
                        gw, u = w2
                        c = u // GB
                        dve.wait_ge(oT_hi_done, at(gw, UNITS // 2, u // 2))
                        nc.vector.tensor_tensor(two_units(oT_lo[:, c], u),
                                                two_units(ps_oT[(u // 2) % 2], 2 * ((u // 2) % 2) + 1),
                                                two_units(oT_hi[:, c], u).bitcast(F32), ALU.subtract).then_inc(oT_lo_done, 1)
                    if nxt and s >= 7:
                        qk_lo(g + 1, s - 7)
                    if s in (8, 9) and not cur and nxt:
                        split_weight(s - 6)
                    if cur and s == 0:
                        qk_lo(g, 5)
                    if cur and 1 <= s <= 3:
                        v_copy(g, s - 1, prev)
                    if prev and cur and s in (5, 6):
                        residual(g - 1, 2 * (s - 5) + 1)
                    if prev and cur and 5 <= s < 5 + GB:
                        statistics(g - 1, s - 5)
                    if cur:
                        dve.wait_ge(logits_done, at(g, UNITS, s))
                        nc.vector.tensor_reduce(abs_max[:, s % E_RING], neg_logits[:, s % A_RING], AX_X, ALU.max,
                                                apply_absolute_value=True).then_inc(abs_done, 1)
                    if prev and cur and 5 <= s < 5 + GB:
                        mean_and_variance(g - 1, s - 5)
                    if prev and cur and s == 8:
                        var_plus_eps(g - 1, 0, GB, var_eps_done)
                    if nxt and s == 4 and cur:
                        dve.wait_ge(xT_loaded, (g + 1) * 16)
                        dve.wait_ge(v_product, at(g, GB, GB - 1))
                        for kc in range(NC):
                            nc.vector.tensor_copy(xT_hi[:, kc], xT_raw[:, kc]).then_inc(xT_hi_done, 1)
                        if not prev:
                            early_xT_lo(g + 1)
                    for b in {9: (0,), 10: (1, 2), 11: (3,)}.get(s, ()) if prev and cur else ():
                        dve.wait_ge(inv_std_done, at(g - 1, 1, 0))
                        normalise(g - 1, b)
                if not cur and prev:
                    last_layer_norms(g - 1)

            bodies(dve, body)

        @block.tensor
        def _(pe):
            def three_passes(ps, stationary, moving, lo_ready=None, very_first=False):
                (s_hi, s_lo), (m_hi, m_lo) = stationary, moving
                pairs = [(s_hi, m_hi), (s_lo, m_hi), (s_hi, m_lo)]
                for n, (a, b) in enumerate(pairs):
                    if n == 2 and lo_ready:
                        pe.wait_ge(*lo_ready)
                    if n == 1 and very_first:
                        pe.wait_ge(w_split_lo, 1)
                    for kc in range(NC):
                        if n == 0 and very_first:
                            pe.wait_ge(xT_hi_done, kc + 1)
                        last = pe.matmul(ps, a(kc), b(kc), start=(n == 0 and kc == 0),
                                         stop=(n == 2 and kc == NC - 1))
                return last

            def project_qk(g, i, first=False, very_first=False):
                c, is_q = divmod(i, 2)
                w = "q" if is_q else "k"
                cols = slice(c * P, (c + 1) * P)
                three_passes(ps_proj[i % 2][:],
                             (lambda kc: w_hi[w][:, kc, cols], lambda kc: w_lo[w][:, kc, cols]),
                             (lambda kc: xT_hi[:, kc], lambda kc: xT_lo[:, kc]),
                             lo_ready=(xT_lo_done, at(g, NC, NC - 1)) if first else None,
                             very_first=very_first).then_inc(qk_product, 1)

            def project_v(g, b):
                nodes = slice(b * N, (b + 1) * N)
                three_passes(ps_proj[b % 2][:, 0:HID],
                             (lambda kc: xT_hi[:, kc, nodes], lambda kc: xT_lo[:, kc, nodes]),
                             (lambda kc: w_hi["v"][:, kc], lambda kc: w_lo["v"][:, kc])).then_inc(v_product, 1)

            def project_out(g, b):
                pe.wait_ge(oT_lo_done, at(g, UNITS // 2, UNITS // 2 - 2 + b // 2))
                nodes = slice(b * N, (b + 1) * N)
                three_passes(ps_proj[b % 2][:, 0:HID],
                             (lambda kc: oT_hi[:, kc, nodes], lambda kc: oT_lo[:, kc, nodes]),
                             (lambda kc: w_hi["o"][:, kc], lambda kc: w_lo["o"][:, kc])).then_inc(out_product, 1)

            def last_project_out(g, b, kc):
                bank = LAST_OUT_BANKS[b]
                if kc == 0:
                    pe.wait_ge(*((y_done, at(g - 1, GB, b + 2)) if b < 2 else (logits_done, at(g, UNITS, UNITS - 4 + b))))
                pe.wait_ge(oT_lo_done, at(g, UNITS // 2, 2 * kc + b // 2))
                nodes = slice(b * N, (b + 1) * N)
                for n, (o_part, w_part) in enumerate(((oT_hi, w_hi), (oT_lo, w_hi), (oT_hi, w_lo))):
                    last = pe.matmul(bank[:, 0:HID], o_part[:, kc, nodes], w_part["o"][:, kc],
                                     start=(kc == 0 and n == 0), stop=(kc == NC - 1 and n == 2))
                if kc == NC - 1:
                    last.then_inc(out_product, 1)

            def scores(g, u, prev):
                c, b = divmod(u, GB)
                if b == 0:
                    pe.wait_ge(k_moved[c], (g + 1) * 16 * K_MOVES)
                    pe.wait_ge(q_moved[c], (g + 1) * 16 * Q_MOVES)
                if u >= 2 or prev:
                    pe.wait_ge(logits_done, at(g, UNITS, u - 2))
                for pair in range(PAIRS):
                    cols = slice(pair * 2 * N, (pair + 1) * 2 * N)
                    for part in range(2):
                        last = pe.matmul(ps_scores[u % 2][:, cols], q_stack[:, c, part, pair, b * N:(b + 1) * N],
                                         k_stack[c][:, pair, b].rearrange("p j m -> p (j m)"),
                                         start=(part == 0), stop=(part == 1))
                last.then_inc(scores_done, 1)

            def transposes(g, u, first):
                pe.wait_ge(probs_scaled, at(g, UNITS, u))
                if not first:
                    pe.wait_ge(probs_T_done, at(g, UNITS, u - 2))
                for h in range(HC):
                    last = pe.transpose(ps_probsT[u % 2][:, h * N:(h + 1) * N], probs[:, u % E_RING, h], ident[:])
                last.then_inc(transposed, 1)

            def values(g, u, first):
                c, b = divmod(u, GB)
                pe.wait_ge(probs_T_done, at(g, UNITS, u))
                if c == 0:
                    pe.wait_ge(v_done, at(g, GB, b))
                half = (u // 2) % 2
                if u % 2 == 0 and not first:
                    pe.wait_ge(oT_lo_done, at(g, UNITS // 2, u // 2 - 2))
                col = (2 * half + u % 2) * N
                for h in range(HC):
                    ch = (c * HC + h) * HD
                    last = pe.matmul(ps_oT[half][h * HD:(h + 1) * HD, col:col + N], v[:, b, ch:ch + HD],
                                     probs_T[:, u % PS_RING, h], start=True, stop=True)
                last.then_inc(values_done, 1)

            OUT_SLOTS = {4: (0, 1), 5: (2, 3)}
            LAST_OUT = {9: ((0, 0),), 10: ((1, 0),), 11: ((0, 1), (1, 1))}
            AFTER_LAST_OUT = {0: ((2, 0),), 1: ((2, 1), (3, 0)), 2: ((3, 1),),
                              3: tuple((b, NC - 1) for b in range(GB))}

            def body(g, prev, cur, nxt):
                for s in range(UNITS):
                    if cur:
                        scores(g, s, prev)
                    for step in (values, transposes) if prev and nxt else (transposes, values):
                        lag, ring = (PV_LAG, 4) if step is values else (T_LAG, 2)
                        if w := unit(g, s - lag, prev, cur):
                            step(*w, first=w[0] is g and not prev and w[1] < ring)
                    if cur and s < GB:
                        b = s
                        if b < 2:
                            pe.wait_ge(qk_lo_done, at(g, 2 * NC, 4 + b))
                        else:
                            pe.wait_ge(v_done, at(g, GB, b - 2))
                        if b == 0:
                            pe.wait_ge(w_split_lo, 3)
                        project_v(g, b)
                    for b in OUT_SLOTS.get(s, ()) if prev and cur else ():
                        if b >= 2:
                            pe.wait_ge(y_done, at(g - 1, GB, b - 2))
                        else:
                            pe.wait_ge(v_done, at(g, GB, b + 2))
                        if b == 0:
                            pe.wait_ge(w_split_lo, 4)
                        project_out(g - 1, b)
                    if not nxt:
                        for b, kc in (LAST_OUT if cur else AFTER_LAST_OUT).get(s, ()):
                            last_project_out(g if cur else g - 1, b, kc)
                    if nxt and s >= 6:
                        i = s - 6
                        if i >= 2:
                            pe.wait_ge(qk_lo_done, at(g + 1, 2 * NC, i - 2))
                        elif prev:
                            pe.wait_ge(y_done, at(g - 1, GB, i + 2))
                        elif cur:
                            pe.wait_ge(v_done, at(g, GB, i + 2))
                        elif i == 0:
                            pe.wait_ge(w_split_hi, 1)
                        else:
                            pe.wait_ge(w_split_lo, i + 1)
                        if i == 0 and cur:
                            pe.wait_ge(xT_hi_done, at(g + 1, NC, NC - 1))
                        project_qk(g + 1, i, first=(i == 0), very_first=(i == 0 and not cur))

            pe.wait_ge(consts_ready, 3)
            bodies(pe, body)


def kernel(x, adj, L0_gnn_Wq, L0_gnn_Wk, L0_gnn_Wv, L0_gnn_bv, L0_gnn_Wo, L0_gnn_bo):
    import numpy as np
    import concourse.bacc as bacc
    from concourse.bass_utils import run_bass_kernel_spmd

    x = np.ascontiguousarray(x)
    graphs, n, hid = x.shape
    xT = x.reshape(graphs // GB, GB, n, hid // 128, 128).transpose(0, 4, 3, 1, 2)
    arrays = {
        "x": x,
        "xT": np.ascontiguousarray(xT).reshape(graphs // GB, 128, hid // 128, GB * n),
        "adj": np.ascontiguousarray(adj),
        "wqT": np.ascontiguousarray(np.asarray(L0_gnn_Wq).T),
        "wkT": np.ascontiguousarray(np.asarray(L0_gnn_Wk).T),
        "wvT": np.ascontiguousarray(np.asarray(L0_gnn_Wv).T),
        "woT": np.ascontiguousarray(np.asarray(L0_gnn_Wo).T),
        "bv": np.ascontiguousarray(L0_gnn_bv),
        "bo": np.ascontiguousarray(L0_gnn_bo),
    }
    nc = bacc.Bacc("TRN2", target_bir_lowering=False, num_devices=1)
    args = [nc.dram_tensor(f"in_{name}", a.shape, mybir.dt.from_np(a.dtype), kind="ExternalInput").ap()
            for name, a in arrays.items()]
    args.append(nc.dram_tensor("out", x.shape, F32, kind="ExternalOutput").ap())
    graph_attention(nc, *args)
    r = run_bass_kernel_spmd(nc, [{f"in_{name}": a for name, a in arrays.items()}], core_ids=[0])
    return r.results[0]["out"]
```
